# Optimizing a Trainium2 kernel written in Bass

```python
import numpy as np
import jax
import jax.numpy as jnp

def _softmax(x, axis=-1):
    return jax.nn.softmax(x, axis=axis)

def _gelu(x):
    return jax.nn.gelu(x, approximate=True)

def _silu(x):
    return jax.nn.silu(x)

def _sigmoid(x):
    return jax.nn.sigmoid(x)

def _layernorm(x, axis=-1, eps=1e-05):
    m = jnp.mean(x, axis=axis, keepdims=True)
    v = jnp.var(x, axis=axis, keepdims=True)
    return (x - m) / jnp.sqrt(v + eps)

def _scatter_add(tgt, idx, src, axis=0):
    return tgt.at[idx].add(src)

def _segment_sum(src, seg, n):
    return jax.ops.segment_sum(src, seg, n)
kernel_name = 'mk_early_fusion_d1_tok_img256_r4_4d4e48'

def setup_inputs(seed: int=0):
    np.random.seed(seed)
    _w = jnp.asarray

    def _rec_inputs():
        import jax
        import jax.numpy as jnp
        _rk = jax.random.key(seed)
        x = -0.000596345 + 1.00056 * jax.random.normal(jax.random.fold_in(_rk, 1), (32, 64, 64, 3), jnp.float32)
        txt = 0.0279957 + 0.402868 * jax.random.normal(jax.random.fold_in(_rk, 2), (32, 128, 64), jnp.float32)
        return (x, txt)
    x, txt = _rec_inputs()

    def _L0_tok_setup():
        import jax, jax.numpy as jnp
        import numpy as np
        M1, M2, WIDTH, LAYERS = (16, 16, 64, 4)
        B, H, W = (16, 64, 64)
        EPS = 1e-05

        def _spectral_conv(h, w1, w2):
            xf = jnp.fft.rfft2(h)
            top = jnp.einsum('bixy,ioxy->boxy', xf[:, :, :M1, :M2], w1)
            bot = jnp.einsum('bixy,ioxy->boxy', xf[:, :, -M1:, :M2], w2)
            of = jnp.zeros(xf.shape, dtype=xf.dtype)
            of = of.at[:, :, :M1, :M2].set(top)
            of = of.at[:, :, -M1:, :M2].set(bot)
            return jnp.fft.irfft2(of, s=(h.shape[-2], h.shape[-1]))
        key = jax.random.key(seed)
        ks = jax.random.split(key, 16)
        scale = 1.0 / (WIDTH * WIDTH)
        inp = {'x': jax.random.normal(ks[0], (B, H, W, 3), dtype=jnp.float32), 'fc0_w': jax.random.normal(ks[1], (3, WIDTH), dtype=jnp.float32) * 0.3, 'fc0_b': jnp.zeros((WIDTH,), jnp.float32), 'w1r': jax.random.normal(ks[2], (LAYERS, WIDTH, WIDTH, M1, M2), dtype=jnp.float32) * scale, 'w1i': jax.random.normal(ks[3], (LAYERS, WIDTH, WIDTH, M1, M2), dtype=jnp.float32) * scale, 'w2r': jax.random.normal(ks[4], (LAYERS, WIDTH, WIDTH, M1, M2), dtype=jnp.float32) * scale, 'w2i': jax.random.normal(ks[5], (LAYERS, WIDTH, WIDTH, M1, M2), dtype=jnp.float32) * scale, 'pw_w': jax.random.normal(ks[6], (LAYERS, WIDTH, WIDTH), dtype=jnp.float32) * (1.0 / np.sqrt(WIDTH)), 'pw_b': jnp.zeros((LAYERS, WIDTH), jnp.float32), 'gamma': jnp.ones((LAYERS, WIDTH), jnp.float32), 'beta': jnp.zeros((LAYERS, WIDTH), jnp.float32), 'fc1_w': jax.random.normal(ks[7], (WIDTH, 128), dtype=jnp.float32) * (1.0 / np.sqrt(WIDTH)), 'fc1_b': jnp.zeros((128,), jnp.float32), 'fc2_w': jax.random.normal(ks[8], (128, 1), dtype=jnp.float32) * (1.0 / np.sqrt(128.0)), 'fc2_b': jnp.zeros((1,), jnp.float32)}
        return inp
    _L0_tok_all = _L0_tok_setup()
    _L0_tok_in = {k: v for k, v in _L0_tok_all.items() if k in ('fc0_w', 'fc0_b', 'w1r', 'w1i', 'w2r', 'w2i', 'pw_w', 'pw_b', 'gamma', 'beta', 'fc1_w', 'fc1_b', 'fc2_w', 'fc2_b')}
    del _L0_tok_all

    def _L0_attn_setup():
        import jax, jax.numpy as jnp
        import numpy as np
        NHEAD = 8
        ATT_EPS = 1e-06
        LN_EPS = 1e-05

        def _layernorm(x, g, b):
            mu = jnp.mean(x, axis=-1, keepdims=True)
            var = jnp.mean(jnp.square(x - mu), axis=-1, keepdims=True)
            return (x - mu) * jax.lax.rsqrt(var + LN_EPS) * g + b
        key = jax.random.key(seed)
        ks = jax.random.split(key, 7)
        N, L, C = (4, 4096, 64)
        s = 1.0 / np.sqrt(C)
        return {'x': jax.random.normal(ks[0], (N, L, C), jnp.float32), 'Wq': jax.random.normal(ks[1], (C, C), jnp.float32) * s, 'Wk': jax.random.normal(ks[2], (C, C), jnp.float32) * s, 'Wv': jax.random.normal(ks[3], (C, C), jnp.float32) * s, 'Wm': jax.random.normal(ks[4], (C, C), jnp.float32) * s, 'W1': jax.random.normal(ks[5], (2 * C, 2 * C), jnp.float32) * (1.0 / np.sqrt(2 * C)), 'W2': jax.random.normal(ks[6], (2 * C, C), jnp.float32) * (1.0 / np.sqrt(2 * C)), 'g1': jnp.ones((C,), jnp.float32), 'b1': jnp.zeros((C,), jnp.float32), 'g2': jnp.ones((C,), jnp.float32), 'b2': jnp.zeros((C,), jnp.float32)}
    _L0_attn_all = _L0_attn_setup()
    _L0_attn_in = {k: v for k, v in _L0_attn_all.items() if k in ('Wq', 'Wk', 'Wv', 'Wm', 'W1', 'W2', 'g1', 'b1', 'g2', 'b2')}
    del _L0_attn_all

    def _L0_ffn_setup():
        import jax, jax.numpy as jnp
        import numpy as np
        C = 64
        EPS = 1e-05
        N_ITERS = 30

        def _layernorm(x, w, bias):
            mu = jnp.mean(x, axis=-1, keepdims=True)
            var = jnp.mean(jnp.square(x - mu), axis=-1, keepdims=True)
            return (x - mu) * jax.lax.rsqrt(var + EPS) * w + bias
        key = jax.random.key(seed)
        kx, kw, kb, klw, klb = jax.random.split(key, 5)
        x = jax.random.normal(kx, (8, 512, C), dtype=jnp.float32)
        bound = 1.0 / np.sqrt(C)
        W = jax.random.uniform(kw, (C, C), minval=-bound, maxval=bound, dtype=jnp.float32)
        b = jax.random.uniform(kb, (C,), minval=-bound, maxval=bound, dtype=jnp.float32)
        ln_w = jnp.ones((C,), dtype=jnp.float32)
        ln_b = jnp.zeros((C,), dtype=jnp.float32)
        return {'x': x, 'ln_w': ln_w, 'ln_b': ln_b, 'W': W, 'b': b}
    _L0_ffn_all = _L0_ffn_setup()
    _L0_ffn_in = {k: v for k, v in _L0_ffn_all.items() if k in ('ln_w', 'ln_b', 'W', 'b')}
    del _L0_ffn_all
    return {'x': x, 'txt': txt, 'L0_tok_fc0_w': _L0_tok_in['fc0_w'], 'L0_tok_fc0_b': _L0_tok_in['fc0_b'], 'L0_tok_w1r': _L0_tok_in['w1r'], 'L0_tok_w1i': _L0_tok_in['w1i'], 'L0_tok_w2r': _L0_tok_in['w2r'], 'L0_tok_w2i': _L0_tok_in['w2i'], 'L0_tok_pw_w': _L0_tok_in['pw_w'], 'L0_tok_pw_b': _L0_tok_in['pw_b'], 'L0_tok_gamma': _L0_tok_in['gamma'], 'L0_tok_beta': _L0_tok_in['beta'], 'L0_tok_fc1_w': _L0_tok_in['fc1_w'], 'L0_tok_fc1_b': _L0_tok_in['fc1_b'], 'L0_tok_fc2_w': _L0_tok_in['fc2_w'], 'L0_tok_fc2_b': _L0_tok_in['fc2_b'], 'L0_attn_Wq': _L0_attn_in['Wq'], 'L0_attn_Wk': _L0_attn_in['Wk'], 'L0_attn_Wv': _L0_attn_in['Wv'], 'L0_attn_Wm': _L0_attn_in['Wm'], 'L0_attn_W1': _L0_attn_in['W1'], 'L0_attn_W2': _L0_attn_in['W2'], 'L0_attn_g1': _L0_attn_in['g1'], 'L0_attn_b1': _L0_attn_in['b1'], 'L0_attn_g2': _L0_attn_in['g2'], 'L0_attn_b2': _L0_attn_in['b2'], 'L0_ffn_ln_w': _L0_ffn_in['ln_w'], 'L0_ffn_ln_b': _L0_ffn_in['ln_b'], 'L0_ffn_W': _L0_ffn_in['W'], 'L0_ffn_b': _L0_ffn_in['b']}

def reference(x, txt, L0_tok_fc0_w, L0_tok_fc0_b, L0_tok_w1r, L0_tok_w1i, L0_tok_w2r, L0_tok_w2i, L0_tok_pw_w, L0_tok_pw_b, L0_tok_gamma, L0_tok_beta, L0_tok_fc1_w, L0_tok_fc1_b, L0_tok_fc2_w, L0_tok_fc2_b, L0_attn_Wq, L0_attn_Wk, L0_attn_Wv, L0_attn_Wm, L0_attn_W1, L0_attn_W2, L0_attn_g1, L0_attn_b1, L0_attn_g2, L0_attn_b2, L0_ffn_ln_w, L0_ffn_ln_b, L0_ffn_W, L0_ffn_b):
    import jax
    import jax.numpy as jnp

    def _L0_tok_ref(x, fc0_w, fc0_b, w1r, w1i, w2r, w2i, pw_w, pw_b, gamma, beta, fc1_w, fc1_b, fc2_w, fc2_b):
        import jax, jax.numpy as jnp
        import numpy as np
        M1, M2, WIDTH, LAYERS = (16, 16, 64, 4)
        B, H, W = (16, 64, 64)
        EPS = 1e-05

        def _spectral_conv(h, w1, w2):
            xf = jnp.fft.rfft2(h)
            top = jnp.einsum('bixy,ioxy->boxy', xf[:, :, :M1, :M2], w1)
            bot = jnp.einsum('bixy,ioxy->boxy', xf[:, :, -M1:, :M2], w2)
            of = jnp.zeros(xf.shape, dtype=xf.dtype)
            of = of.at[:, :, :M1, :M2].set(top)
            of = of.at[:, :, -M1:, :M2].set(bot)
            return jnp.fft.irfft2(of, s=(h.shape[-2], h.shape[-1]))
        h = jnp.einsum('bhwi,ic->bhwc', x, fc0_w) + fc0_b
        h = h.transpose(0, 3, 1, 2)
        for l in range(LAYERS):
            sc = _spectral_conv(h, w1r[l] + 1j * w1i[l], w2r[l] + 1j * w2i[l])
            pw = jnp.einsum('bihw,oi->bohw', h, pw_w[l]) + pw_b[l][None, :, None, None]
            y = sc + pw
            mean = y.mean(axis=(0, 2, 3), keepdims=True)
            var = y.var(axis=(0, 2, 3), keepdims=True)
            y = (y - mean) * jax.lax.rsqrt(var + EPS)
            y = y * gamma[l][None, :, None, None] + beta[l][None, :, None, None]
            h = jax.nn.gelu(y, approximate=False)
        h = h.transpose(0, 2, 3, 1)
        h = jax.nn.gelu(h @ fc1_w + fc1_b, approximate=False)
        out = (h @ fc2_w + fc2_b).squeeze(-1)
        return out

    def _L0_attn_ref(x, Wq, Wk, Wv, Wm, W1, W2, g1, b1, g2, b2):
        import jax, jax.numpy as jnp
        import numpy as np
        NHEAD = 8
        ATT_EPS = 1e-06
        LN_EPS = 1e-05

        def _layernorm(x, g, b):
            mu = jnp.mean(x, axis=-1, keepdims=True)
            var = jnp.mean(jnp.square(x - mu), axis=-1, keepdims=True)
            return (x - mu) * jax.lax.rsqrt(var + LN_EPS) * g + b
        N, L, C = x.shape
        H = NHEAD
        D = C // H
        q = (x @ Wq).reshape(N, L, H, D)
        k = (x @ Wk).reshape(N, L, H, D)
        v = (x @ Wv).reshape(N, L, H, D)
        Q = jax.nn.elu(q) + 1.0
        K = jax.nn.elu(k) + 1.0
        v = v / L
        KV = jnp.einsum('nshd,nshv->nhdv', K, v)
        Z = 1.0 / (jnp.einsum('nlhd,nhd->nlh', Q, K.sum(axis=1)) + ATT_EPS)
        msg = jnp.einsum('nlhd,nhdv,nlh->nlhv', Q, KV, Z) * L
        msg = msg.reshape(N, L, C) @ Wm
        msg = _layernorm(msg, g1, b1)
        h = jnp.concatenate([x, msg], axis=-1) @ W1
        h = jax.nn.relu(h) @ W2
        msg = _layernorm(h, g2, b2)
        return x + msg

    def _L0_ffn_ref(x, ln_w, ln_b, W, b):
        import jax, jax.numpy as jnp
        import numpy as np
        C = 64
        EPS = 1e-05
        N_ITERS = 30

        def _layernorm(x, w, bias):
            mu = jnp.mean(x, axis=-1, keepdims=True)
            var = jnp.mean(jnp.square(x - mu), axis=-1, keepdims=True)
            return (x - mu) * jax.lax.rsqrt(var + EPS) * w + bias

        def step(h, _):
            h = h + 0.01 * jnp.tanh(h)
            h = h * jax.nn.sigmoid(h)
            h = _layernorm(h, ln_w, ln_b)
            h = jnp.einsum('bsc,dc->bsd', h, W) + b
            return (h, None)
        x, _ = jax.lax.scan(step, x, None, length=N_ITERS)
        return x
    h = _L0_tok_ref(x, L0_tok_fc0_w, L0_tok_fc0_b, L0_tok_w1r, L0_tok_w1i, L0_tok_w2r, L0_tok_w2i, L0_tok_pw_w, L0_tok_pw_b, L0_tok_gamma, L0_tok_beta, L0_tok_fc1_w, L0_tok_fc1_b, L0_tok_fc2_w, L0_tok_fc2_b)
    h = jnp.concatenate([h, txt], axis=1)
    h = h + _L0_attn_ref(_layernorm(h, axis=-1), L0_attn_Wq, L0_attn_Wk, L0_attn_Wv, L0_attn_Wm, L0_attn_W1, L0_attn_W2, L0_attn_g1, L0_attn_b1, L0_attn_g2, L0_attn_b2)
    h = h + _L0_ffn_ref(_layernorm(h, axis=-1), L0_ffn_ln_w, L0_ffn_ln_b, L0_ffn_W, L0_ffn_b)
    return h

_drawn_inputs = setup_inputs


def setup_inputs(seed=0):
    import zlib

    import numpy as np

    out = dict(_drawn_inputs(seed))
    spreads = {'L0_tok_fc0_b': (0.0, 0.8),
     'L0_tok_pw_b': (0.0, 0.8),
     'L0_tok_gamma': (1.0, 0.2),
     'L0_tok_beta': (0.0, 0.1),
     'L0_tok_fc1_b': (0.0, 0.1),
     'L0_attn_g1': (1.0, 0.2),
     'L0_attn_b1': (0.0, 0.1),
     'L0_attn_g2': (1.0, 0.2),
     'L0_attn_b2': (0.0, 0.1),
     'L0_ffn_ln_w': (1.0, 0.2),
     'L0_ffn_ln_b': (0.0, 0.1)}
    factors = {'L0_tok_w1r': 8.0, 'L0_tok_w1i': 8.0, 'L0_tok_w2r': 8.0, 'L0_tok_w2i': 8.0}
    for name, (base, spread) in spreads.items():
        noise = np.random.default_rng([zlib.crc32(name.encode()), seed]).standard_normal(out[name].shape)
        drawn = base * np.exp(spread * noise) if base else spread * noise
        out[name] = jnp.asarray(drawn.astype(out[name].dtype))
    for name, factor in factors.items():
        out[name] = (out[name] * factor).astype(out[name].dtype)
    return out
```

```python
import numpy as np

B, H, W, C, LAYERS = 32, 64, 64, 64, 4
MODES = 16
KX, KY = 2 * MODES, MODES
NQ = 8
NK = 8
CH = 1024
HID = 128
TXT = 128
EPS = 1e-5
RSQRT_SEED = 0x5F3759DF


def first(L):
    return isinstance(L, int) and L == 0


def build_tokenizer(nc, t, hcat):
    import concourse.bass as bass
    from concourse import mybir
    from contextlib import ExitStack

    F32, I32 = mybir.dt.float32, mybir.dt.int32
    ALU, ACT = mybir.AluOpType, mybir.ActivationFunctionType
    ds = bass.ds
    ydram = nc.dram_tensor("y_scratch", [NQ * NK, 128, CH], F32, kind="Internal").ap()

    with ExitStack() as ctx:
        def sb(name, shape, dt=F32):
            return ctx.enter_context(nc.sbuf_tensor(name, shape, dt))

        def sem(name):
            return ctx.enter_context(nc.semaphore(name))

        XY = sb("modes", [128, KX * KY * B])
        WM = sb("mode_weights", [128, 2, 4096])
        ARENA = sb("arena", [128, 16384])
        YC = sb("y_in", [128, 4, CH])
        X1 = sb("row_modes", [128, 4096])
        C1 = sb("c_w_forward", [128, 2, 128])
        C2 = sb("c_h_forward", [128, 2, 128])
        C3 = sb("c_h_inverse", [128, 2, 128])
        C4 = sb("c_w_inverse", [128, 256])
        ID = sb("c_identity", [128, 128])
        AV = sb("c_average", [128, 128])
        PW = sb("pointwise_w", [128, 128])
        FC0 = sb("fc0_w", [6, 128])
        FC0B = sb("fc0_b", [128, 1])
        PRM = sb("layer_params", [128, 3])
        FC1 = sb("fc1_w", [128, 2, HID])
        FC1B = sb("fc1_b", [HID, 1])
        FC2P = sb("fc2_w", [HID, 63])
        FC2B = sb("fc2_b", [32, 1])
        BN = sb("bn_stats", [128, 128, 6])
        MV = sb("bn_small", [128, 16])
        SS = sb("bn_scale_shift", [128, 2])
        XT = [ARENA[:, i * 8192:(i + 1) * 8192] for i in range(2)]
        XC = [ARENA[:, i * 4096:(i + 1) * 4096].rearrange("p (m f b) -> p m f b", f=2, b=B) for i in range(2)]
        YQ = [ARENA[:, i * 2048:(i + 1) * 2048] for i in range(2)]
        T3 = ARENA[:, 4096:6144]
        S4 = [ARENA[:, 8192 + i * 4096:8192 + (i + 1) * 4096] for i in range(2)]
        YO = [X1[:, i * CH:(i + 1) * CH] for i in range(4)]
        G = [ARENA[:, i * CH:(i + 1) * CH] for i in range(4)]
        TO = ARENA[0:32, 8192:8704]
        XIN = [ARENA[0:6, i * CH:(i + 1) * CH] for i in range(4)]

        PS = [ctx.enter_context(nc.psum_tensor(f"ps{i}", [128, 1024], F32)) for i in range(4)]
        psA, psB = PS[0:2], PS[2:4]
        psT = [PS[0][:, 0:512], PS[0][:, 512:1024]]
        psS = [PS[1][:, 0:512], PS[1][:, 512:1024]]
        psY = PS[2:4]

        s_const = sem("const_loaded")
        s_zero = sem("zeroed")
        s_pwl = sem("pointwise_w_loaded")
        s_prm = sem("params_loaded")
        s_yl = [sem(f"chunk_loaded{i}") for i in range(4)]
        s_xin = [sem(f"image_loaded{i}") for i in range(4)]
        s_f0 = sem("fc0_done")
        F0_CREDIT = 4
        s_f0e = sem("fc0_read")
        F0E_CREDIT = 2
        s_pst = [sem(f"h0_stored{i}") for i in range(4)]
        s_hc = sem("chunk_activated")
        s_xt = sem("chunk_transposed")
        s_s1 = sem("w_transform_done")
        S1_CREDIT = 8
        s_s1e = sem("w_transform_read")
        S1E_CREDIT = 2
        s_s2 = sem("h_transform_done")
        S2_CREDIT = 2
        s_s2e = sem("h_transform_read")
        S2E_CREDIT = 8
        s_wl = [sem(f"mode_w_loaded{i}") for i in range(2)]
        s_xa = sem("form_a_ready")
        s_xlo = sem("form_b_low_ready")
        s_xhi = sem("form_b_high_ready")
        s_mx = sem("mode_products_done")
        MX_CREDIT = 4
        s_mxe = sem("mode_products_read")
        MXE_CREDIT = 4
        s_yq = sem("quad_modes_staged")
        s_t3 = sem("mode_transpose_done")
        T3_CREDIT = 8
        s_t3e = sem("mode_transpose_read")
        T3E_CREDIT = 2
        s_s3 = sem("h_inverse_done")
        S3_CREDIT = 1
        s_s3e = sem("h_inverse_transposed")
        S3E_CREDIT = 2
        s_y = sem("y_done")
        Y_CREDIT = 16
        s_ye = sem("y_read")
        YE_CREDIT = 2
        s_bn = sem("bn_stats_done")
        BN_CREDIT = 4
        s_st = [sem(f"chunk_stored{i}") for i in range(4)]
        ST_CREDIT = 16
        s_sm = sem("bn_small_step")
        s_av = sem("bn_average_done")
        s_ss = sem("scale_shift_ready")
        s_f1 = sem("hidden_done")
        s_f1e = sem("hidden_activated")
        F1E_CREDIT = 2
        s_f2 = sem("head_unit_done")
        F2_CREDIT = 4
        s_to = sem("head_read")
        TO_CREDIT = 2
        s_ts = sem("tokens_stored")
        TS_CREDIT = 128
        s_txt = sem("text_copied")

        block = ctx.enter_context(nc.Block())
        NCONST = 13
        SMALL = 22

        def loaded(L, phase, q, k):
            return 16 * (L * 32 + phase * 16 + q * 2 + k // 4 + 1)

        @block.sync
        def _(eng):
            for s in s_st:
                eng.nop().then_inc(s, ST_CREDIT)
            eng.nop().then_inc(s_ts, TS_CREDIT)
            for dst, src in ((C1[:, :, :], t["c1"]), (C2[:, :, :], t["c2"]), (C3[:, :, :], t["c3"]),
                             (C4[:, :], t["c4"]), (ID[:, :], t["ident"]), (AV[:, :], t["avg"]),
                             (FC0B[0:64, :], t["fc0_b"]), (FC0B[64:128, :], t["fc0_b"]),
                             (FC1B[:, :], t["fc1_b"]), (FC2B[:, :], t["fc2_b"].broadcast_to((32, 1)))):
                eng.dma_start(dst, src).then_inc(s_const, 16)
            eng.wait_ge(s_zero, 4)
            for bp in range(2):
                eng.dma_start(FC0[3 * bp:3 * bp + 3, 64 * bp:64 * bp + 64], t["fc0_w"]).then_inc(s_const, 16)
                eng.dma_start(FC1[64 * bp:64 * bp + 64, bp, :], t["fc1_w"]).then_inc(s_const, 16)
            eng.dma_start(FC2P[:, 31:32], t["fc2_w"]).then_inc(s_const, 16)
            with eng.Fori(0, NQ) as q:
                for k in range(NK):
                    eng.wait_ge(s_f0, q * NK + k + 1)
                    eng.dma_start(XIN[k % 4], t["x"][q * NK + k]).then_inc(s_xin[k % 4], 16)
            for k in range(4):
                eng.wait_ge(s_pst[k], ST_CREDIT + 16 * 16)

            def load(q, k):
                eng.dma_start(YC[:, k % 4, :], ydram[q * NK + k]).then_inc(s_yl[k % 4], 16)

            def passes(free, base, per, store=None):
                for k in range(4):
                    load(0, k)

                def quad(q, last):
                    for k in range(NK):
                        if not (last and k >= 4):
                            eng.wait_ge(free, base + per * (q * NK + k + 1))
                            load(q + (k + 4) // NK, (k + 4) % NK)
                        if store is not None:
                            store(q, k)

                with eng.Fori(0, NQ - 1) as q:
                    quad(q, False)
                quad(NQ - 1, True)

            def mode_weights(L, c):
                eng.wait_ge(s_mx, L * 16 + 2 * c + 2)
                eng.dma_start(WM[:, c % 2, :], t["modew"][L * 8 + c]).then_inc(s_wl[c % 2], 16)

            def layer(L):
                if not first(L):
                    for k in range(4):
                        eng.wait_ge(s_st[k], ST_CREDIT + L * 256)
                    eng.wait_ge(s_ss, L)
                for bp in range(2):
                    eng.dma_start(PW[64 * bp:64 * bp + 64, 64 * bp:64 * bp + 64], t["pw_w"][L]).then_inc(s_pwl, 16)
                    eng.dma_start(PRM[64 * bp:64 * bp + 64, :], t["prm"][L]).then_inc(s_prm, 16)
                mode_weights(L, 0)
                mode_weights(L, 1)
                passes(s_xt, L * 64, 1)
                for c in range(2, 8):
                    mode_weights(L, c)
                eng.wait_ge(s_xt, L * 64 + 64)

                def store(q, k):
                    eng.wait_ge(s_ye, YE_CREDIT + L * 64 + q * NK + k + 1)
                    eng.dma_start(ydram[q * NK + k], YO[k % 4]).then_inc(s_st[k % 4], 16)

                passes(s_y, Y_CREDIT + L * 64, 1, store)

            layer(0)
            with eng.Fori(1, LAYERS) as L:
                layer(L)
            for k in range(4):
                eng.wait_ge(s_st[k], ST_CREDIT + LAYERS * 256)
            hv = hcat.rearrange("(q z bp) s w -> q z bp s w", z=2, bp=2)

            def store_tokens(q, k):
                if k < NK - 1:
                    return
                eng.wait_ge(s_to, TO_CREDIT + q + 1)
                for bp in range(2):
                    for z in range(2):
                        for hh in range(2):
                            src = TO[bp * 16:bp * 16 + 16, :]\
                                .rearrange("r (h z hh w) -> r h z hh w", h=2, z=2, hh=2)[:, :, z, hh, :]
                            dst = hv[q, z, bp, hh * 32:hh * 32 + 32, :].rearrange("(r h) w -> r h w", h=2)
                            eng.dma_start(dst, src).then_inc(s_ts, 16)

            passes(s_f1, 0, 2, store_tokens)
            eng.wait_ge(s_ts, TS_CREDIT + NQ * 128)

        @block.gpsimd
        def _(eng):
            eng.memset(PW[:, :], 0.0).then_inc(s_zero, 1)
            eng.memset(FC0[:, :], 0.0).then_inc(s_zero, 1)
            eng.memset(FC1[:, :, :], 0.0).then_inc(s_zero, 1)
            eng.memset(FC2P[:, :], 0.0).then_inc(s_zero, 1)
            eng.dma_start(hcat[:, H:H + TXT, :], t["txt"]).then_inc(s_txt, 16)
            xyb = XY[:, :].rearrange("p (m b) -> p m b", b=B)
            yv = XY[:, :].rearrange("p (kx kyp ri b) -> p kyp b kx ri", kx=KX, kyp=8, ri=2)
            yqv = [y.rearrange("p (kyp b kx ri) -> p kyp b kx ri", kyp=8, b=4, kx=KX) for y in YQ]

            def layer(L):
                with eng.Fori(0, 4) as h:
                    for i in range(2):
                        c = h * 2 + i
                        eng.wait_ge(s_s2e, S2E_CREDIT + L * 64 + 64)
                        eng.wait_ge(s_mx, L * 16 + c * 2 + 2)
                        eng.tensor_copy(XC[i][:, :, 0, :], xyb[:, ds(c * 64, 64), :]).then_inc(s_xa, 1)
                with eng.Fori(0, 4) as h:
                    for i in range(2):
                        q = h * 2 + i
                        eng.wait_ge(s_mxe, MXE_CREDIT + L * 16 + 16)
                        eng.wait_ge(s_t3, (L * NQ + q) * 4 + 4)
                        for kyp in range(8):
                            for ri in range(2):
                                eng.tensor_copy(yqv[i][:, kyp, :, :, ri], yv[:, kyp, ds(q * 4, 4), :, ri])\
                                   .then_inc(s_yq, 1)

            layer(0)
            with eng.Fori(1, LAYERS) as L:
                layer(L)
            eng.wait_ge(s_txt, 16)

        @block.tensor
        def _(pe):
            for s, credit in ((s_f0, F0_CREDIT), (s_s1, S1_CREDIT), (s_s2, S2_CREDIT), (s_mx, MX_CREDIT),
                              (s_t3, T3_CREDIT), (s_s3, S3_CREDIT), (s_y, Y_CREDIT), (s_f2, F2_CREDIT)):
                pe.nop().then_inc(s, credit)
            pe.wait_ge(s_const, 16 * 15)
            with pe.Fori(0, NQ) as q:
                for k in range(NK):
                    pe.wait_ge(s_xin[k % 4], 16 * (q * 2 + k // 4 + 1))
                    pe.wait_ge(s_f0e, q * NK + k + 1)
                    for half in range(2):
                        last = pe.matmul(psA[k % 2][:, half * 512:half * 512 + 512], FC0[:, :],
                                         XIN[k % 4][:, half * 512:half * 512 + 512], start=True, stop=True)
                    last.then_inc(s_f0, 1)

            xts = [x.rearrange("p (r wh c) -> p r wh c", wh=2, c=32) for x in XT]
            x1s = X1[:, :].rearrange("p (m k) -> p m k", k=32)
            t3s = T3.rearrange("p (z kk o) -> p o z kk", z=2, kk=16)
            s4s = [x.rearrange("p (m r) -> p m r", r=32) for x in S4]

            def forward(L, q, i):
                pe.wait_ge(s_xt, L * 64 + (q + 1) * NK)
                for g in range(4):
                    pe.wait_ge(s_s1e, (L * NQ + q) * 4 + g + 1)
                    for cc in range(8):
                        for wh in range(2):
                            last = pe.matmul(psA[g % 2][:, cc * 128:cc * 128 + 128], xts[i][:, :, wh, g * 8 + cc],
                                             C1[:, wh, :], start=(wh == 0), stop=(wh == 1))
                    last.then_inc(s_s1, 1)
                pe.wait_ge(s_s1e, S1E_CREDIT + (L * NQ + q + 1) * 4)
                for g in range(2):
                    pe.wait_ge(s_s2e, (L * NQ + q) * 8 + g * 4 + 4)
                    for j in range(8):
                        for ri in range(2):
                            last = pe.matmul(psB[g][:, j * 128:j * 128 + 128], x1s[:, :, ri * KY + g * 8 + j],
                                             C2[:, ri, :], start=(ri == 0), stop=(ri == 1))
                    last.then_inc(s_s2, 1)

            def modes(L, c, i, first):
                pe.wait_ge(s_wl[i], 16 * (L * 4 + first + 1))
                pe.wait_ge(s_xa, L * 8 + c + 1)
                pe.wait_ge(s_xlo, L * 8 + c + 1)
                pe.wait_ge(s_xhi, L * 8 + c + 1)
                for u in range(2):
                    pe.wait_ge(s_mxe, L * 16 + c * 2 + u + 1)
                    for x in range(2):
                        for y in range(KY):
                            m = (u * 2 + x) * KY + y
                            at = x * 512 + (y % 8) * 64
                            last = pe.matmul(PS[i * 2 + u][(y // 8) * 64:(y // 8) * 64 + 64, at:at + 64],
                                             WM[:, i, m * 64:m * 64 + 64],
                                             XC[i][:, m, :, :].rearrange("p f b -> p (f b)"), start=True, stop=True)
                    last.then_inc(s_mx, 1)

            def turn(L, q, i, g):
                Q = L * NQ + q
                if g == 0:
                    pe.wait_ge(s_yq, (Q + 1) * 16)
                pe.wait_ge(s_t3e, Q * 4 + g + 1)
                for j in range(4):
                    at = ((g % 2) * 4 + j) * 256 + (g // 2) * 128
                    last = pe.transpose(psT[g % 2][:, j * 128:j * 128 + 128], YQ[i][:, at:at + 128], ID[:, :])
                last.then_inc(s_t3, 1)

            def rows(L, q, g):
                Q = L * NQ + q
                if g == 0:
                    pe.wait_ge(s_t3e, T3E_CREDIT + (Q + 1) * 4)
                pe.wait_ge(s_s3e, Q * 8 + g + 1)
                pe.matmul(psS[g % 2], C3[:, g // 4, :], t3s[:, (g % 4) * 16:(g % 4) * 16 + 16, :, :],
                          start=True, stop=True).then_inc(s_s3, 1)

            def sums(L, q, i, k):
                Q = L * NQ + q
                if k == 0:
                    pe.wait_ge(s_s3e, S3E_CREDIT + (Q + 1) * 8)
                pe.wait_ge(s_hc, L * 128 + 64 + q * NK + k + 1)
                pe.wait_ge(s_ye, Q * NK + k + 1)
                for half in range(2):
                    at = half * 512
                    pe.matmul(psY[k % 2][:, at:at + 512], PW[:, :], YC[:, k % 4, at:at + 512], start=True, stop=False)
                    for j in range(2):
                        last = pe.matmul(psY[k % 2][:, at + j * 256:at + j * 256 + 256],
                                         s4s[i][:, :, k * 4 + half * 2 + j], C4[:, :], start=False, stop=(j == 1))
                last.then_inc(s_y, 1)

            def inverse(L, q, i, prepare, finish):
                for k in range(NK):
                    if finish:
                        sums(L, q - 1, 1 - i, k)
                    if prepare and k < 4:
                        turn(L, q, i, k)
                    if prepare and k >= 4:
                        rows(L, q, (k - 4) * 2)
                        rows(L, q, (k - 4) * 2 + 1)

            def layer(L):
                with pe.Fori(0, 4) as h:
                    for i in range(2):
                        forward(L, h * 2 + i, i)
                with pe.Fori(0, 4) as h:
                    for i in range(2):
                        modes(L, h * 2 + i, i, h)
                pe.wait_ge(s_pwl, 32 * (L + 1))
                inverse(L, 0, 0, True, False)
                with pe.Fori(0, 3) as h:
                    inverse(L, h * 2 + 1, 1, True, True)
                    inverse(L, h * 2 + 2, 0, True, True)
                inverse(L, 7, 1, True, True)
                inverse(L, 8, 0, False, True)
                pe.wait_ge(s_sm, L * SMALL + 1)
                pe.matmul(psT[0][:, 0:1], AV[:, :], MV[:, 0:1], start=True, stop=True).then_inc(s_av, 1)
                pe.wait_ge(s_sm, L * SMALL + 4)
                pe.matmul(psT[0][:, 1:2], AV[:, :], MV[:, 4:5], start=True, stop=True).then_inc(s_av, 1)

            layer(0)
            with pe.Fori(1, LAYERS) as L:
                layer(L)

            def head2(q, i, k):
                for bp in range(2):
                    n = q * 16 + k * 2 + bp
                    pe.wait_ge(s_f1e, F1E_CREDIT + n + 1)
                    for half in range(2):
                        r = bp * 16 + k * 2 + half
                        last = pe.matmul(psB[i][0:32, 0:512], FC2P[:, 31 - r:63 - r],
                                         G[(k % 2) * 2 + bp][:, half * 512:half * 512 + 512],
                                         start=(k == 0 and r == 0), stop=(k == NK - 1 and r == 31))
                    last.then_inc(s_f2, 1)

            with pe.Fori(0, 4) as h:
                for i in range(2):
                    q = h * 2 + i
                    pe.wait_ge(s_to, q + 1)
                    for k in range(NK):
                        pe.wait_ge(s_hc, LAYERS * 128 + q * NK + k + 1)
                        for bp in range(2):
                            pe.wait_ge(s_f1e, q * 16 + k * 2 + bp + 1)
                            for half in range(2):
                                last = pe.matmul(psA[bp][:, half * 512:half * 512 + 512], FC1[:, bp, :],
                                                 YC[:, k % 4, half * 512:half * 512 + 512], start=True, stop=True)
                            last.then_inc(s_f1, 1)
                        if k > 0:
                            head2(q, i, k - 1)
                    head2(q, i, NK - 1)

        @block.scalar
        def _(act):
            for s, credit in ((s_f0e, F0E_CREDIT), (s_s1e, S1E_CREDIT), (s_mxe, MXE_CREDIT), (s_t3e, T3E_CREDIT),
                              (s_ye, YE_CREDIT), (s_f1e, F1E_CREDIT)):
                act.nop().then_inc(s, credit)
            for s in s_pst:
                act.nop().then_inc(s, ST_CREDIT)
            act.wait_ge(s_const, 16 * 15)
            with act.Fori(0, NQ) as q:
                for k in range(NK):
                    act.wait_ge(s_f0, F0_CREDIT + q * NK + k + 1)
                    act.wait_ge(s_pst[k % 4], 16 * (q * 2 + k // 4) + 16)
                    act.activation(YC[:, k % 4, :], psA[k % 2][:, :], ACT.Identity, bias=FC0B[:, 0:1]).then_inc(s_f0e, 1)
                    act.wait_ge(s_f0e, F0E_CREDIT + q * NK + k + 1)
                    act.dma_start(ydram[q * NK + k], YC[:, k % 4, :]).then_inc(s_pst[k % 4], 16)

            x1o = X1[:, :].rearrange("p (cb c k) -> p c cb k", cb=4, c=32)
            xyb = XY[:, :].rearrange("p (m b) -> p m b", b=B)

            def activate(L, phase, q, k):
                act.wait_ge(s_yl[k % 4], loaded(L, phase, q, k))
                if first(L):
                    act.nop().then_inc(s_hc, 1)
                else:
                    act.activation(YC[:, k % 4, :], YC[:, k % 4, :], ACT.Gelu, bias=SS[:, 1:2],
                                   scale=SS[:, 0:1]).then_inc(s_hc, 1)

            def read_s1(L, q):
                for g in range(4):
                    act.wait_ge(s_s1, S1_CREDIT + (L * NQ + q) * 4 + g + 1)
                    if g == 0:
                        act.wait_ge(s_s2, (L * NQ + q) * 2 + 2)
                    act.activation(x1o[:, g * 8:g * 8 + 8, :, :],
                                   psA[g % 2][:, :].rearrange("p (c cb k) -> p c cb k", c=8, cb=4),
                                   ACT.Copy).then_inc(s_s1e, 1)

            def high(L, c, i):
                act.wait_ge(s_mx, L * 16 + c * 2 + 2)
                act.activation(XC[i][64:128, :, 1, :], xyb[0:64, ds(c * 64, 64), :], ACT.Copy).then_inc(s_xhi, 1)

            def read_modes(L, c, i):
                for u in range(2):
                    act.wait_ge(s_mx, MX_CREDIT + L * 16 + c * 2 + u + 1)
                    act.activation(XY[:, ds(c * 2048 + u * 1024, 1024)], PS[i * 2 + u][:, :], ACT.Copy).then_inc(s_mxe, 1)

            def read_turned(L, q, g):
                Q = L * NQ + q
                act.wait_ge(s_t3, T3_CREDIT + Q * 4 + g + 1)
                if g == 0:
                    act.wait_ge(s_s3, Q * 8 + 1)
                act.activation(T3[:, g * 512:g * 512 + 512], psT[g % 2], ACT.Copy).then_inc(s_t3e, 1)

            def read_sum(L, q, k):
                n = L * 64 + q * NK + k
                act.wait_ge(s_y, Y_CREDIT + n + 1)
                act.wait_ge(s_st[k % 4], 16 * (L * 16 + q * 2 + k // 4) + 16)
                act.wait_ge(s_bn, n + 1)
                act.activation(YO[k % 4], psY[k % 2][:, :], ACT.Identity, bias=PRM[:, 2:3]).then_inc(s_ye, 1)

            def inverse(L, q, prepare, finish, ends):
                for k in range(NK):
                    if finish and not (ends and k == NK - 1):
                        activate(L, 1, q - 1 + (k + 1) // NK, (k + 1) % NK)
                    if finish:
                        read_sum(L, q - 1, k)
                    if prepare and k < 4:
                        read_turned(L, q, k)

            def layer(L):
                if not first(L):
                    act.wait_ge(s_ss, L)
                    for k in range(4):
                        act.wait_ge(s_st[k], ST_CREDIT + L * 256)
                for k in range(NK):
                    activate(L, 0, 0, k)
                with act.Fori(0, NQ - 1) as q:
                    for k in range(NK):
                        activate(L, 0, q + 1, k)
                    read_s1(L, q)
                read_s1(L, NQ - 1)
                act.wait_ge(s_s2e, S2E_CREDIT + L * 64 + 64)
                high(L, 0, 0)
                high(L, 1, 1)
                with act.Fori(0, 3) as h:
                    for i in range(2):
                        read_modes(L, h * 2 + i, i)
                        high(L, h * 2 + i + 2, i)
                for i in range(2):
                    read_modes(L, 6 + i, i)
                act.wait_ge(s_prm, 32 * (L + 1))
                inverse(L, 0, True, False, False)
                activate(L, 1, 0, 0)
                with act.Fori(1, NQ) as q:
                    inverse(L, q, True, True, False)
                inverse(L, NQ, False, True, True)

            layer(0)
            with act.Fori(1, LAYERS) as L:
                layer(L)

            def hidden(q, k):
                for bp in range(2):
                    n = q * 16 + k * 2 + bp
                    act.wait_ge(s_f1, n + 1)
                    act.wait_ge(s_f2, n + 1)
                    act.activation(G[(k % 2) * 2 + bp], psA[bp][:, :], ACT.Gelu, bias=FC1B[:, 0:1]).then_inc(s_f1e, 1)

            act.wait_ge(s_ss, LAYERS)
            activate(LAYERS, 0, 0, 0)
            with act.Fori(0, NQ - 1) as q:
                for k in range(NK):
                    activate(LAYERS, 0, q + (k + 1) // NK, (k + 1) % NK)
                    hidden(q, k)
            for k in range(NK):
                if k < NK - 1:
                    activate(LAYERS, 0, NQ - 1, k + 1)
                hidden(NQ - 1, k)

        @block.vector
        def _(dve):
            for s, credit in ((s_s2e, S2E_CREDIT), (s_s3e, S3E_CREDIT), (s_bn, BN_CREDIT), (s_to, TO_CREDIT)):
                dve.nop().then_inc(s, credit)
            xo = XY[:, :].rearrange("p (kx ky q z bp) -> p q bp ky z kx", kx=KX, ky=KY, q=NQ, z=2)
            xyb = XY[:, :].rearrange("p (m b) -> p m b", b=B)

            def transposes(L, q, i):
                for k in range(NK):
                    dve.wait_ge(s_hc, L * 128 + q * NK + k + 1)
                    if k == 0:
                        dve.wait_ge(s_s1, (L * NQ + q) * 4 + 4)
                    dve.transpose(XT[i][:, k * CH:k * CH + CH], YC[:, k % 4, :]).then_inc(s_xt, 1)

            def read_s2(L, q):
                for g in range(2):
                    dve.wait_ge(s_s2, S2_CREDIT + (L * NQ + q) * 2 + g + 1)
                    for bp in range(2):
                        src = psB[g][bp * 64:bp * 64 + 64, :].rearrange("p (ky ri z kx) -> p ri ky z kx", ky=8, ri=2, z=2)
                        for ri in range(2):
                            dve.tensor_copy(xo[ri * 64:ri * 64 + 64, q, bp, g * 8:g * 8 + 8, :, :],
                                            src[:, ri, :, :, :]).then_inc(s_s2e, 1)

            def low(L, c, i):
                dve.wait_ge(s_s2e, S2E_CREDIT + L * 64 + 64)
                dve.wait_ge(s_mx, L * 16 + c * 2 + 2)
                dve.tensor_scalar(XC[i][0:64, :, 1, :], xyb[64:128, ds(c * 64, 64), :], -1.0, None,
                                  ALU.mult).then_inc(s_xlo, 1)

            def read_rows(L, q, i, g):
                Q = L * NQ + q
                dve.wait_ge(s_s3, S3_CREDIT + Q * 8 + g + 1)
                if g == 0:
                    dve.wait_ge(s_y, Q * 8 + 8)
                dve.transpose(S4[i][:, g * 512:g * 512 + 512], psS[g % 2]).then_inc(s_s3e, 1)

            def stats(L, q, k):
                n = L * 64 + q * NK + k
                dve.wait_ge(s_ye, YE_CREDIT + n + 1)
                dve.bn_stats(BN[:, ds(q * 16 + k * 2, 1), :].rearrange("p a s -> p (a s)"), YO[k % 4][:, 0:512])
                dve.bn_stats(BN[:, ds(q * 16 + k * 2 + 1, 1), :].rearrange("p a s -> p (a s)"),
                             YO[k % 4][:, 512:1024]).then_inc(s_bn, 1)

            def inverse(L, q, i, prepare, finish):
                for k in range(NK):
                    if finish:
                        stats(L, q - 1, k)
                    if prepare and k >= 4:
                        read_rows(L, q, i, (k - 4) * 2)
                        read_rows(L, q, i, (k - 4) * 2 + 1)

            def scale_shift(L):
                base = L * SMALL
                steps = [0]

                def step(instruction):
                    instruction.then_inc(s_sm, 1)
                    steps[0] += 1
                    dve.wait_ge(s_sm, base + steps[0])

                def col(i):
                    return MV[:, i:i + 1]

                dve.wait_ge(s_bn, BN_CREDIT + L * 64 + 64)
                dve.memset(MV[:, 15:16], 0.0)
                step(dve.bn_aggr(MV[:, 0:2], BN[:, :, :].rearrange("p n s -> p (n s)")))
                dve.wait_ge(s_av, 2 * L + 1)
                step(dve.tensor_copy(col(2), psT[0][:, 0:1]))
                step(dve.tensor_tensor(col(3), col(0), col(2), ALU.subtract))
                step(dve.scalar_tensor_tensor(out=col(4), in0=col(3), scalar=col(3), in1=col(1),
                                              op0=ALU.mult, op1=ALU.add))
                dve.wait_ge(s_av, 2 * L + 2)
                step(dve.tensor_scalar(col(5), psT[0][:, 1:2], EPS, None, ALU.add))
                step(dve.tensor_scalar(col(6).bitcast(I32), col(5).bitcast(I32), 1, None, ALU.logical_shift_right))
                step(dve.tensor_scalar(col(6).bitcast(I32), col(6).bitcast(I32), -1, RSQRT_SEED, ALU.mult, ALU.add))
                for _ in range(4):
                    step(dve.scalar_tensor_tensor(out=col(7), in0=col(6), scalar=-0.5, in1=col(6),
                                                  op0=ALU.mult, op1=ALU.mult))
                    step(dve.tensor_tensor(col(7), col(7), col(5), ALU.mult))
                    step(dve.scalar_tensor_tensor(out=col(6), in0=col(7), scalar=1.5, in1=col(6),
                                                  op0=ALU.add, op1=ALU.mult))
                dve.wait_ge(s_prm, 32 * (L + 1))
                step(dve.tensor_tensor(SS[:, 0:1], col(6), PRM[:, 0:1], ALU.mult))
                step(dve.tensor_tensor(col(8), col(2), SS[:, 0:1], ALU.mult))
                step(dve.tensor_tensor(SS[:, 1:2], PRM[:, 1:2], col(8), ALU.subtract))
                assert steps[0] == SMALL
                dve.nop().then_inc(s_ss, 1)

            def layer(L):
                transposes(L, 0, 0)
                with dve.Fori(0, 3) as h:
                    for i in range(2):
                        transposes(L, h * 2 + i + 1, 1 - i)
                        read_s2(L, h * 2 + i)
                transposes(L, 7, 1)
                read_s2(L, 6)
                read_s2(L, 7)
                with dve.Fori(0, 4) as h:
                    for i in range(2):
                        low(L, h * 2 + i, i)
                inverse(L, 0, 0, True, False)
                with dve.Fori(0, 3) as h:
                    inverse(L, h * 2 + 1, 1, True, True)
                    inverse(L, h * 2 + 2, 0, True, True)
                inverse(L, 7, 1, True, True)
                inverse(L, 8, 0, False, True)
                scale_shift(L)

            layer(0)
            with dve.Fori(1, LAYERS) as L:
                layer(L)
            dve.wait_ge(s_const, 16 * 15)
            with dve.Fori(0, 4) as h:
                for i in range(2):
                    q = h * 2 + i
                    dve.wait_ge(s_f2, F2_CREDIT + (q + 1) * 16)
                    dve.wait_ge(s_ts, 128 * q + TS_CREDIT)
                    dve.tensor_scalar(TO, psB[i][0:32, 0:512], FC2B[:, 0:1], None, ALU.add).then_inc(s_to, 1)


def build_mixer(nc, t, hcat, out):
    import concourse.bass as bass
    from concourse import mybir
    from contextlib import ExitStack

    F32, I32 = mybir.dt.float32, mybir.dt.int32
    ALU, ACT, AX = mybir.AluOpType, mybir.ActivationFunctionType, mybir.AxisListType
    L = H + TXT
    NT = B * L // 128
    NP = NT // 2
    NG = 6
    ITERS = 30
    ATT_EPS = 1e-6

    with ExitStack() as ctx:
        def sb(name, shape, dt=F32):
            return ctx.enter_context(nc.sbuf_tensor(name, shape, dt))

        def sem(name):
            return ctx.enter_context(nc.semaphore(name))

        HT = sb("tokens", [128, NT, C])
        XN = sb("tokens_normed", [128, NT, C])
        XNT = sb("tokens_normed_t", [128, NP, 128])
        QT = sb("queries_t", [128, NP, 128])
        KE = sb("keys", [128, NT, C])
        VE = sb("values", [128, NT, C + 1])
        VH = sb("values_halved", [128, 2, NT // 3, C + 1])
        KVM = sb("key_value", [128, B, 2, 128])
        MS = sb("message", [128, NT, C])
        MT = sb("message_t", [128, NP, 128])
        D = sb("centered", [128, NT, C])
        E = sb("work", [128, NT, C])
        HIDT = sb("hidden_t", [128, 2, NP, 128])
        ST = sb("row_stats", [128, 8, NT])
        WQ = sb("w_q", [128, 128])
        WKV = sb("w_kv", [128, 256])
        WMB = sb("w_m", [128, 128])
        W1X = sb("w_1_x", [128, 128])
        W1M = sb("w_1_m", [128, 128])
        W2 = sb("w_2", [128, C])
        GB = sb("gains", [128, 5, C])
        ID = sb("c_identity2", [128, 128])
        MASK = sb("c_heads", [128, 2, C])
        HALF = sb("c_halves", [128, 2])
        CEN = sb("c_center", [128, 128])
        WF = sb("w_ffn_t", [128, 128])
        LNW = sb("ffn_ln_w", [128, 1])
        LNB = sb("ffn_ln_b", [64, 1])
        LNBR = sb("ffn_ln_b_rows", [64, 128])
        WA = sb("w_ffn_scaled", [128, 128])
        RW = sb("w_ffn_centered", [128, 2, 65])
        MC = sb("c_mean_columns", [128, 2])
        BF = sb("ffn_bias", [128, C])
        PM = ctx.enter_context(nc.psum_tensor("pm", [128, 8 * 512], F32))
        PS = [PM[:, i * 512:i * 512 + 512] for i in range(8)]
        FY = [PM[:, i:i + 1024].rearrange("p (k r) -> p k r", k=2)[:, :, 0:390].rearrange("p k (j c) -> p k j c", c=65)
              for i in (2048, 3072)]

        s_in = sem("mixer_inputs_loaded")
        s_z = sem("mixer_zeroed")
        s_dve = sem("dve_step")
        s_ln = [sem(f"ln{i}_centered") for i in range(4)]
        s_sq = [sem(f"ln{i}_squared") for i in range(4)]
        s_xn = sem("x_normed")
        s_xt = sem("x_turned")
        s_xte = sem("x_turned_read")
        s_kv = sem("kv_done")
        s_kvm = sem("k_clipped")
        s_kx = sem("k_exp_done")
        s_ke = sem("keys_ready")
        s_ve = sem("values_ready")
        s_q = sem("q_done")
        s_qm = sem("q_clipped")
        s_qx = sem("q_exp_done")
        s_qe = sem("queries_ready")
        s_c = sem("contexts_done")
        s_ce = sem("contexts_ready")
        s_m = sem("messages_done")
        s_me = sem("messages_ready")
        s_mt = sem("messages_turned")
        s_mte = sem("messages_turned_read")
        s_p = sem("messages_projected")
        s_pn = sem("messages_normed")
        s_pt = sem("normed_turned")
        s_pte = sem("normed_turned_read")
        s_h = sem("hidden_done2")
        s_he = sem("hidden_read2")
        s_o = sem("w2_done")
        s_wf = sem("ffn_weights")
        s_wfe = sem("ffn_weights_ready")
        s_r = sem("ffn_input_ready")
        s_th = sem("ffn_tanh")
        s_hp = sem("ffn_nudged")
        s_sg = sem("ffn_sigmoid")
        s_s = sem("ffn_gated")
        s_s2 = sem("ffn_squared")
        s_ft = sem("ffn_turned")
        s_fy = sem("ffn_product")
        s_sc = sem("ffn_scaled")
        s_ms = sem("ffn_mean_squared")
        s_ftr = sem("ffn_turned_read")
        FTE_CREDIT = 4
        FY_CREDIT = 4
        s_fs = sem("ffn_small_step")
        s_pn2 = sem("w2_normed")
        s_res = sem("residual_added")
        s_fin = sem("result_ready")
        s_out = sem("out_stored")
        NIN = 29
        SMALL2 = 12
        PARTS = 4
        PT = NT // PARTS
        block = ctx.enter_context(nc.Block())

        def grp(x, g):
            return x[:, g * 8:g * 8 + 8, :]

        def bank(g):
            return PS[g][:, :].rearrange("p (t c) -> p t c", c=C)

        def pairs(x, g):
            return x[:, g * 4:g * 4 + 4, :].rearrange("p i t -> p (i t)")

        @block.sync
        def _(eng):
            eng.dma_start(HT[:, :, :], hcat.rearrange("b s c -> (b s) c").rearrange("(t p) c -> p t c", p=128)).then_inc(s_in, 16)
            eng.wait_ge(s_z, 4)
            for g in range(2):
                a = slice(64 * g, 64 * g + 64)
                for dst, src in ((WQ[a, a], "Wq"), (WKV[a, a], "Wk"), (WKV[a, 128 + 64 * g:192 + 64 * g], "Wv"),
                                 (WMB[a, a], "Wm"), (WF[a, a], "ffn_wt"), (LNW[a, :], "ln_w")):
                    eng.dma_start(dst, t[src]).then_inc(s_in, 16)
                eng.dma_start(W1X[a, :], t["W1"][0:64, :]).then_inc(s_in, 16)
                eng.dma_start(W1M[a, :], t["W1"][64:128, :]).then_inc(s_in, 16)
            for i, n in enumerate(("g1", "b1", "g2", "b2", "ffn_b")):
                eng.dma_start(GB[:, i, :], t[n].broadcast_to((128, C))).then_inc(s_in, 16)
            for dst, src in ((W2[:, :], t["W2"]), (ID[:, :], t["ident"]), (MASK[:, :, :], t["heads"]), (HALF[:, :], t["halves"]), (CEN[:, :], t["center"]),
                             (MC[:, :], t["meancol"])):
                eng.dma_start(dst, src).then_inc(s_in, 16)
            eng.dma_start(LNB[:, :], t["ln_b"]).then_inc(s_in, 16)
            eng.wait_ge(s_fin, NG)
            eng.dma_start(out.rearrange("b s c -> (b s) c").rearrange("(t p) c -> p t c", p=128), HT[:, :, :]).then_inc(s_out, 16)
            eng.wait_ge(s_out, 16)

        @block.gpsimd
        def _(eng):
            eng.memset(WQ[:, :], 0.0).then_inc(s_z, 1)
            eng.memset(WKV[:, :], 0.0).then_inc(s_z, 1)
            eng.memset(WMB[:, :], 0.0).then_inc(s_z, 1)
            eng.memset(WF[:, :], 0.0).then_inc(s_z, 1)
            eng.memset(VE[:, :, C:C + 1], 1.0).then_inc(s_z, 1)
            eng.wait_ge(s_xn, 2 * NG)
            eng.wait_ge(s_wfe, 1)
            eng.nop().then_inc(s_r, PARTS)
            bias = BF[:, :].rearrange("p (o c) -> p o c", o=1).broadcast_to((128, PT, C))
            with eng.Fori(0, ITERS) as n:
                for k in range(PARTS):
                    eng.wait_ge(s_sc, PARTS * n + k + 1)
                    x = XN[:, k * PT:(k + 1) * PT, :]
                    eng.tensor_tensor(x, x, bias, ALU.add).then_inc(s_r, 1)

        def span(b):
            m, j = b // 2, 3 * (b // 2)
            full, i = (j, 0) if b % 2 == 0 else (j + 2, 1)
            return [(KE[:, full, :], VE[:, full, :]), (KE[:, j + 1, :], VH[:, i, m, :])]

        @block.tensor
        def _(pe):
            pe.wait_ge(s_in, 16 * NIN)
            for g in range(NG):
                pe.wait_ge(s_xn, g + 1)
                if g >= 2:
                    pe.wait_ge(s_xte, g - 1)
                for i in range(4):
                    last = pe.transpose(PS[6 + g % 2][:, i * 128:i * 128 + 128],
                                        XN[:, g * 8 + 2 * i:g * 8 + 2 * i + 2, :].rearrange("p t c -> p (t c)"), ID[:, :])
                last.then_inc(s_xt, 1)
            for u in range(2 * NG):
                if u % 2 == 0:
                    pe.wait_ge(s_xte, u // 2 + 1)
                if u >= 6:
                    pe.wait_ge(s_ke, u - 5)
                    pe.wait_ge(s_ve, u - 5)
                for i in range(2):
                    last = pe.matmul(PS[u % 6][:, i * 256:i * 256 + 256], XNT[:, u * 2 + i, :], WKV[:, :], start=True, stop=True)
                last.then_inc(s_kv, 1)
            for g in range(NG):
                if g >= 2:
                    pe.wait_ge(s_qe, g - 1)
                pe.matmul(PS[6 + g % 2][:, :], WQ[:, :], pairs(XNT, g), start=True, stop=True).then_inc(s_q, 1)
            pe.wait_ge(s_ke, 12)
            pe.wait_ge(s_ve, 14)
            for u in range(B // 4):
                if u >= 6:
                    pe.wait_ge(s_ce, 4 * (u - 5))
                for i in range(4):
                    for half in range(2):
                        for n, (k, v) in enumerate(span(u * 4 + i)):
                            last = pe.matmul(PS[u % 6][half * 64:half * 64 + 64, i * 128:i * 128 + 65],
                                             k, v, start=(n == 0), stop=(n == 1))
                last.then_inc(s_c, 1)
            pe.wait_ge(s_ce, B)
            pe.wait_ge(s_qe, NG)
            for u in range(NT // 4):
                if u >= 6:
                    pe.wait_ge(s_me, u - 5)
                for i in range(4):
                    j = u * 4 + i
                    whole = {0: 2 * (j // 3), 2: 2 * (j // 3) + 1}.get(j % 3)
                    o = PS[u % 6][:, i * 128:i * 128 + 128]
                    if whole is not None:
                        last = pe.matmul(o, QT[:, j // 2, :], KVM[:, whole, j % 2, :], start=True, stop=True)
                    else:
                        for n in range(2):
                            last = pe.matmul(o[n * 64:n * 64 + 64, :], QT[:, j // 2, n * 64:n * 64 + 64],
                                             KVM[:, 2 * (j // 3) + n, j % 2, :], start=True, stop=True)
                last.then_inc(s_m, 1)
            for g in range(NG):
                pe.wait_ge(s_me, 2 * g + 2)
                if g >= 2:
                    pe.wait_ge(s_mte, g - 1)
                for i in range(4):
                    last = pe.transpose(PS[6 + g % 2][:, i * 128:i * 128 + 128],
                                        MS[:, g * 8 + 2 * i:g * 8 + 2 * i + 2, :].rearrange("p t c -> p (t c)"), ID[:, :])
                last.then_inc(s_mt, 1)
            pe.wait_ge(s_me, 12)
            for g in range(NG):
                pe.wait_ge(s_mte, g + 1)
                for i in range(4):
                    last = pe.matmul(PS[g][:, i * 128:i * 128 + 128], MT[:, g * 4 + i, :], WMB[:, :], start=True, stop=True)
                last.then_inc(s_p, 1)
            for g in range(NG):
                pe.wait_ge(s_pn, g + 1)
                if g >= 2:
                    pe.wait_ge(s_pte, g - 1)
                for i in range(4):
                    last = pe.transpose(PS[6 + g % 2][:, i * 128:i * 128 + 128],
                                        MS[:, g * 8 + 2 * i:g * 8 + 2 * i + 2, :].rearrange("p t c -> p (t c)"), ID[:, :])
                last.then_inc(s_pt, 1)
            pe.wait_ge(s_pte, NG)
            for u in range(2 * NG):
                g, a = u // 2, 64 * (u % 2)
                if u >= 2:
                    pe.wait_ge(s_he, u - 1)
                pe.matmul(PS[6 + u % 2][:, :], W1X[a:a + 64, :], pairs(XNT[a:a + 64], g), start=True, stop=False)
                pe.matmul(PS[6 + u % 2][:, :], W1M[a:a + 64, :], pairs(MT[a:a + 64], g), start=False, stop=True).then_inc(s_h, 1)
            for g in range(NG):
                pe.wait_ge(s_he, 2 * g + 2)
                for j in range(8):
                    last = pe.matmul(PS[g][:, j * 64:j * 64 + 64], HIDT[:, j % 2, g * 4 + j // 2, :], W2[:, :], start=True, stop=True)
                last.then_inc(s_o, 1)
            pe.wait_ge(s_wf, 2)
            pe.matmul(PS[6][:, 0:128], CEN[:, :], WA[:, :], start=True, stop=True)
            pe.matmul(PS[7][:, 0:64], LNBR[:, :], WF[0:64, 0:64], start=True, stop=True).then_inc(s_wf, 1)
            pe.wait_ge(s_wfe, 1)

            pe.nop().then_inc(s_fy, FY_CREDIT)
            with pe.Fori(0, ITERS) as n:
                for k in range(PARTS):
                    m = PARTS * n + k
                    pe.wait_ge(s_s, m + 1)
                    pe.wait_ge(s_ftr, 2 * m + FTE_CREDIT)
                    for i in range(6):
                        j = k * PT + 2 * i
                        last = pe.transpose(PS[2 * (k % 2) + i // 3][:, (i % 3) * 128:(i % 3) * 128 + 128],
                                            MS[:, j:j + 2, :].rearrange("p t c -> p (t c)"), ID[:, :])
                        if i % 3 == 2:
                            last.then_inc(s_ft, 1)
                    for i in range(6):
                        if i % 3 == 0:
                            pe.wait_ge(s_ftr, FTE_CREDIT + 2 * m + i // 3 + 1)
                        last = pe.matmul(PS[4 + 2 * (k % 2) + i // 3][:, (i % 3) * 130:(i % 3) * 130 + 130],
                                         MT[:, k * 6 + i, :], RW[:, :, :].rearrange("p g c -> p (g c)"), start=True, stop=True)
                    last.then_inc(s_fy, 1)

        @block.scalar
        def _(act):
            act.wait_ge(s_in, 16 * NIN)

            def squares(n):
                for g in range(NG):
                    act.wait_ge(s_ln[n], g + 1)
                    act.activation(grp(E, g), grp(D, g), ACT.Square).then_inc(s_sq[n], 1)

            squares(0)
            for g in range(NG):
                act.wait_ge(s_xt, g + 1)
                act.activation(pairs(XNT, g), PS[6 + g % 2][:, :], ACT.Copy).then_inc(s_xte, 1)
            for u in range(2 * NG):
                act.wait_ge(s_kv, u + 1)
                kv = PS[u % 6][:, :].rearrange("p (i k g c) -> p k i g c", i=2, k=2, g=2)
                act.wait_ge(s_z, 5)
                act.activation(VE[:, u * 4:u * 4 + 4, 0:C].rearrange("p (i g) c -> p i g c", g=2), kv[:, 1], ACT.Copy,
                               scale=1.0 / L).then_inc(s_ve, 1)
                act.wait_ge(s_kvm, u + 1)
                act.activation(E[:, u * 4:u * 4 + 4, :], E[:, u * 4:u * 4 + 4, :], ACT.Exp).then_inc(s_kx, 1)
            act.wait_ge(s_ve, 12)
            for i in range(2):
                act.activation(VH[:, i, :, :], VE[:, :, :].rearrange("p (m a) c -> p m a c", a=3)[:, :, 1, :], ACT.Copy,
                               scale=HALF[:, i:i + 1]).then_inc(s_ve, 1)
            for g in range(NG):
                act.wait_ge(s_qm, g + 1)
                act.activation(grp(D, g), grp(D, g), ACT.Exp).then_inc(s_qx, 1)
            for g in range(NG):
                act.wait_ge(s_mt, g + 1)
                act.activation(pairs(MT, g), PS[6 + g % 2][:, :], ACT.Copy).then_inc(s_mte, 1)
            squares(1)
            for g in range(NG):
                act.wait_ge(s_pt, g + 1)
                act.wait_ge(s_p, NG)
                act.activation(pairs(MT, g), PS[6 + g % 2][:, :], ACT.Copy).then_inc(s_pte, 1)
            for u in range(2 * NG):
                act.wait_ge(s_h, u + 1)
                act.activation(HIDT[:, u % 2, (u // 2) * 4:(u // 2) * 4 + 4, :].rearrange("p i t -> p (i t)"),
                               PS[6 + u % 2][:, :], ACT.Relu).then_inc(s_he, 1)
            squares(2)
            squares(3)

            def part(x, k):
                return x[:, k * PT:(k + 1) * PT, :]

            act.nop().then_inc(s_ftr, FTE_CREDIT)
            act.preload_act_table_set("sigmoid_and_others")

            def tanh(m, k):
                act.wait_ge(s_r, m + 1)
                act.activation(part(D, k), part(XN, k), ACT.Tanh).then_inc(s_th, 1)

            def mean_square(m, k):
                act.wait_ge(s_fy, FY_CREDIT + m + 1)
                act.activation(ST[:, 4, k * PT:(k + 1) * PT].rearrange("p (b j) -> p b j", b=2), FY[k % 2][:, :, :, 64],
                               ACT.Square).then_inc(s_ms, 1)

            def quarter(m, k, before, after):
                act.wait_ge(s_hp, m + 1)
                act.activation(part(E, k), part(D, k), ACT.Sigmoid).then_inc(s_sg, 1)
                if after:
                    tanh(m + 1, (k + 1) % PARTS)
                if before:
                    mean_square(m - 1, (k - 1) % PARTS)
                act.wait_ge(s_s, m + 1)
                act.wait_ge(s_fy, m + 1)
                for i in range(2):
                    act.wait_ge(s_ft, 2 * m + i + 1)
                    act.activation(MT[:, k * 6 + i * 3:k * 6 + i * 3 + 3, :].rearrange("p i t -> p (i t)"),
                                   PS[2 * (k % 2) + i][:, 0:384], ACT.Copy).then_inc(s_ftr, 1)
                act.activation(part(E, k), part(MS, k), ACT.Square).then_inc(s_s2, 1)

            tanh(0, 0)
            for k in range(PARTS):
                quarter(k, k, k > 0, True)
            with act.Fori(1, ITERS - 1) as n:
                for k in range(PARTS):
                    quarter(PARTS * n + k, k, True, True)
            for k in range(PARTS):
                quarter(PARTS * (ITERS - 1) + k, k, True, k < PARTS - 1)
            mean_square(PARTS * ITERS - 1, PARTS - 1)

        @block.vector
        def _(dve):
            steps = [0]

            def step(instruction):
                instruction.then_inc(s_dve, 1)
                steps[0] += 1
                dve.wait_ge(s_dve, steps[0])

            def spread(x, g):
                return x[:, g * 8:g * 8 + 8].rearrange("p (t o) -> p t o", o=1).broadcast_to((128, 8, C))

            def rsqrt(v, y, w, x, do):
                do(dve.tensor_scalar(y.bitcast(I32), v.bitcast(I32), -0.5, float(RSQRT_SEED), ALU.mult, ALU.add))
                do(dve.tensor_tensor(w, y, y, ALU.mult))
                do(dve.tensor_tensor(w, w, v, ALU.mult))
                do(dve.tensor_scalar(x, w, 0.375, -1.25, ALU.mult, ALU.add))
                do(dve.tensor_tensor(w, w, x, ALU.mult))
                do(dve.scalar_tensor_tensor(out=y, in0=w, scalar=1.875, in1=y, op0=ALU.add, op1=ALU.mult))
                do(dve.scalar_tensor_tensor(out=w, in0=y, scalar=-0.5, in1=y, op0=ALU.mult, op1=ALU.mult))
                do(dve.tensor_tensor(w, w, v, ALU.mult))
                do(dve.scalar_tensor_tensor(out=y, in0=w, scalar=1.5, in1=y, op0=ALU.add, op1=ALU.mult))

            def norm(n, src, ready, dst, done, gain=None):
                for g in range(NG):
                    if ready is not None:
                        dve.wait_ge(ready, g + 1)
                    step(dve.tensor_reduce(ST[:, 0, g * 8:g * 8 + 8], src(g), axis=AX.X, op=ALU.add))
                step(dve.tensor_scalar(ST[:, 0, :], ST[:, 0, :], 1.0 / C, None, ALU.mult))
                for g in range(NG):
                    dve.tensor_tensor(grp(D, g), src(g), spread(ST[:, 0, :], g), ALU.subtract).then_inc(s_ln[n], 1)
                for g in range(NG):
                    dve.wait_ge(s_sq[n], g + 1)
                    step(dve.tensor_reduce(ST[:, 1, g * 8:g * 8 + 8], grp(E, g), axis=AX.X, op=ALU.add))
                step(dve.tensor_scalar(ST[:, 2, :], ST[:, 1, :], 1.0 / C, EPS, ALU.mult, ALU.add))
                rsqrt(ST[:, 2, :], ST[:, 3, :], ST[:, 4, :], ST[:, 5, :], step)
                for g in range(NG):
                    r = dve.tensor_tensor(grp(dst, g), grp(D, g), spread(ST[:, 3, :], g), ALU.mult)
                    if gain is not None:
                        step(r)
                        step(dve.tensor_tensor(grp(dst, g), grp(dst, g), GB[:, gain:gain + 1, :].broadcast_to((128, 8, C)), ALU.mult))
                        r = dve.tensor_tensor(grp(dst, g), grp(dst, g), GB[:, gain + 1:gain + 2, :].broadcast_to((128, 8, C)), ALU.add)
                    r.then_inc(done, 1)

            dve.wait_ge(s_in, 16 * NIN)
            norm(0, lambda g: grp(HT, g), None, XN, s_xn)
            dve.wait_ge(s_xn, NG)
            def key_clip(u):
                kv = PS[u % 6][:, :].rearrange("p (i k g c) -> p k i g c", i=2, k=2, g=2)
                dve.wait_ge(s_kv, u + 1)
                dve.wait_ge(s_ve, u + 1)
                dve.tensor_scalar(E[:, u * 4:u * 4 + 4, :].rearrange("p (i g) c -> p i g c", g=2), kv[:, 0], 0.0, None,
                                  ALU.min).then_inc(s_kvm, 1)

            def key_sum(u):
                kv = PS[u % 6][:, :].rearrange("p (i k gc) -> p k i gc", i=2, k=2)
                dve.wait_ge(s_kx, u + 1)
                dve.scalar_tensor_tensor(out=KE[:, u * 4:u * 4 + 4, :].rearrange("p (i g) c -> p i (g c)", g=2), in0=kv[:, 0],
                                         scalar=0.0, in1=E[:, u * 4:u * 4 + 4, :].rearrange("p (i g) c -> p i (g c)", g=2),
                                         op0=ALU.max, op1=ALU.add).then_inc(s_ke, 1)

            key_clip(0)
            for u in range(2 * NG):
                if u + 1 < 2 * NG:
                    key_clip(u + 1)
                key_sum(u)
            for g in range(NG):
                dve.wait_ge(s_q, g + 1)
                q = PS[6 + g % 2][:, :]
                d = grp(D, g).rearrange("p t c -> p (t c)")
                dve.tensor_scalar(d, q, 0.0, None, ALU.min).then_inc(s_qm, 1)
                dve.wait_ge(s_qx, g + 1)
                dve.scalar_tensor_tensor(out=pairs(QT, g), in0=q, scalar=0.0, in1=d, op0=ALU.max, op1=ALU.add).then_inc(s_qe, 1)
            for u in range(B // 4):
                dve.wait_ge(s_c, u + 1)
                src = PS[u % 6][:, :].rearrange("p (b c) -> p b c", b=4)
                for g in range(2):
                    mask = MASK[:, g:g + 1, :].broadcast_to((128, 4, C))
                    kvm = KVM[:, u * 4:u * 4 + 4, g, :]
                    dve.tensor_tensor(kvm[:, :, 0:64], src[:, :, 0:64], mask, ALU.mult).then_inc(s_ce, 1)
                    dve.tensor_tensor(kvm[:, :, 64:128], src[:, :, 64:65].broadcast_to((128, 4, 64)), mask,
                                      ALU.mult).then_inc(s_ce, 1)
            for u in range(NT // 4):
                dve.wait_ge(s_m, u + 1)
                src = PS[u % 6][:, :].rearrange("p (t c) -> p t c", t=4)
                e = E[:, u * 4:u * 4 + 4, :]
                step(dve.tensor_scalar(e, src[:, :, 64:128], ATT_EPS, None, ALU.add))
                step(dve.reciprocal(e, e))
                dve.scalar_tensor_tensor(out=MS[:, u * 4:u * 4 + 4, :], in0=src[:, :, 0:64], scalar=float(L), in1=e,
                                         op0=ALU.mult, op1=ALU.mult).then_inc(s_me, 1)
            dve.wait_ge(s_mte, NG)
            norm(1, bank, s_p, MS, s_pn, gain=0)
            norm(2, bank, s_o, MS, s_pn2, gain=2)
            dve.wait_ge(s_pn2, NG)
            for g in range(NG):
                step(dve.tensor_tensor(grp(HT, g), grp(HT, g), grp(XN, g), ALU.add))
                step(dve.tensor_tensor(grp(HT, g), grp(HT, g), grp(MS, g), ALU.add))
            dve.tensor_scalar(WA[:, :], WF[:, :], LNW[:, 0:1], None, ALU.mult).then_inc(s_wf, 1)
            dve.tensor_copy(LNBR[:, :], LNB[:, 0:1].broadcast_to((64, 128))).then_inc(s_wf, 1)
            dve.wait_ge(s_wf, 3)
            step(dve.tensor_copy(RW[:, :, 0:64], PS[6][:, 0:128].rearrange("p (g c) -> p g c", g=2)))
            step(dve.tensor_copy(RW[:, :, 64], MC[:, :]))
            step(dve.tensor_tensor(BF[:, :], PS[7][:, 0:64], GB[:, 4, :], ALU.add))
            dve.nop().then_inc(s_wfe, 1)
            norm(3, lambda g: grp(HT, g), None, XN, s_xn)

            def part(x, k):
                return x[:, k * PT:(k + 1) * PT, :]

            def nudge(m, k):
                dve.wait_ge(s_th, m + 1)
                dve.scalar_tensor_tensor(out=part(D, k), in0=part(D, k), scalar=0.01, in1=part(XN, k), op0=ALU.mult,
                                         op1=ALU.add).then_inc(s_hp, 1)

            def gate(m, k):
                dve.wait_ge(s_sg, m + 1)
                dve.wait_ge(s_hp, m + 1)
                dve.tensor_tensor(part(MS, k), part(D, k), part(E, k), ALU.mult).then_inc(s_s, 1)

            def rescale(m, k):
                count = [0]

                def do(instruction):
                    instruction.then_inc(s_fs, 1)
                    count[0] += 1
                    dve.wait_ge(s_fs, m * SMALL2 + count[0])

                def st(i):
                    return ST[:, i, k * PT:(k + 1) * PT]

                dve.wait_ge(s_s2, m + 1)
                do(dve.tensor_reduce(st(1), part(E, k), axis=AX.X, op=ALU.add))
                dve.wait_ge(s_ms, m + 1)
                do(dve.scalar_tensor_tensor(out=st(2), in0=st(1), scalar=1.0 / C, in1=st(4), op0=ALU.mult, op1=ALU.subtract))
                do(dve.tensor_scalar(st(2), st(2), 0.0, EPS, ALU.max, ALU.add))
                rsqrt(st(2), st(3), st(6), st(5), do)
                r = st(3).rearrange("p (b j o) -> p b j o", b=2, o=1).broadcast_to((128, 2, 6, C))
                assert count[0] == SMALL2, count[0]
                dve.tensor_tensor(part(XN, k).rearrange("p (b j) c -> p b j c", b=2), FY[k % 2][:, :, :, 0:64], r,
                                  ALU.mult).then_inc(s_sc, 1)

            def quarter(m, k, before):
                nudge(m, k)
                if before:
                    rescale(m - 2, (k - 2) % PARTS)
                gate(m, k)

            for k in range(PARTS):
                quarter(k, k, k >= 2)
            with dve.Fori(1, ITERS) as n:
                for k in range(PARTS):
                    quarter(PARTS * n + k, k, True)
            for k in range(2, PARTS):
                rescale(PARTS * (ITERS - 1) + k, k)
            dve.wait_ge(s_r, PARTS * (ITERS + 1))
            for g in range(NG):
                dve.tensor_tensor(grp(HT, g), grp(HT, g), grp(XN, g), ALU.add).then_inc(s_fin, 1)


def constants():
    f = 2 * np.pi / 64
    ky = np.arange(16)
    kx = np.concatenate([np.arange(16), np.arange(-16, 0)])
    w = np.arange(64)
    c1 = np.zeros((4, 32, 2, 4, 2, 16))
    ang = f * np.outer(w, ky).reshape(2, 32, 16)
    for cb in range(4):
        c1[cb, :, :, cb, 0] = np.cos(ang).transpose(1, 0, 2)
        c1[cb, :, :, cb, 1] = -np.sin(ang).transpose(1, 0, 2)
    ang = f * np.outer(w, kx).reshape(2, 32, 32)
    cs, sn = np.cos(ang), np.sin(ang)
    c2 = np.zeros((32, 2, 2, 2, 2, 2, 32))
    for z in range(2):
        for hh in range(2):
            c2[:, z, hh, 0, 0, z] = cs[hh]
            c2[:, z, hh, 1, 0, z] = sn[hh]
            c2[:, z, hh, 0, 1, z] = sn[hh]
            c2[:, z, hh, 1, 1, z] = -cs[hh]
    c3 = np.zeros((2, 32, 2, 2, 2, 2, 32))
    for bp in range(2):
        for hh in range(2):
            c3[bp, :, 0, bp, 0, hh] = cs[hh].T
            c3[bp, :, 1, bp, 0, hh] = -sn[hh].T
            c3[bp, :, 0, bp, 1, hh] = sn[hh].T
            c3[bp, :, 1, bp, 1, hh] = cs[hh].T
    kk = np.arange(16)
    order = (kk % 2) * 8 + kk // 2
    wt = np.where(order == 0, 1.0, 2.0)[:, None] / 4096
    ang = f * np.outer(order, w)
    c4 = np.zeros((2, 2, 2, 16, 2, 2, 64))
    for z in range(2):
        for hh in range(2):
            c4[0, hh, z, :, z, hh] = wt * np.cos(ang)
            c4[1, hh, z, :, z, hh] = -wt * np.sin(ang)
    p = np.arange(128)
    avg = (p[:, None] % 64 == p[None, :] % 64) * 0.5
    heads = (np.arange(64)[:, None] // 8 == np.arange(64)[None, :] // 8) * 1.0
    heads = np.stack([np.concatenate([heads, 0 * heads]), np.concatenate([0 * heads, heads])], 1)
    center = np.eye(128) - (p[:, None] // 64 == p[None, :] // 64) / 64
    meancol = (p[:, None] // 64 == np.arange(2)[None, :]) / 64
    r = lambda a, *s: np.ascontiguousarray(a.reshape(s), dtype=np.float32)
    return {"c1": r(c1, 128, 2, 128), "c2": r(c2, 128, 2, 128), "c3": r(c3, 128, 2, 128), "c4": r(c4, 128, 256),
            "ident": r(np.eye(128), 128, 128), "avg": r(avg, 128, 128),
            "heads": r(heads, 128, 2, 64), "halves": r(p[:, None] // 64 == np.arange(2)[None, :], 128, 2), "center": r(center, 128, 128), "meancol": r(meancol, 128, 2)}


def laid_out(i):
    g = {k: np.asarray(v) for k, v in i.items()}
    x = g["x"].reshape(8, 2, 2, 2, 8, 4, 64, 3).transpose(0, 4, 2, 7, 5, 1, 3, 6).reshape(64, 6, 1024)
    def pack(a):
        return np.asarray(a).reshape(4, 64, 64, 4, 4, 16).transpose(0, 3, 1, 4, 5, 2)
    top = np.stack([pack(g["L0_tok_w1r"]), pack(g["L0_tok_w1i"])], 2)
    bot = np.stack([pack(g["L0_tok_w2r"]), pack(g["L0_tok_w2i"])], 2)
    modew = np.stack([top, bot], 1).reshape(32, 128, 4096)
    c = np.ascontiguousarray
    return {"x": c(x), "txt": g["txt"], "modew": c(modew),
            "fc0_w": g["L0_tok_fc0_w"], "fc0_b": g["L0_tok_fc0_b"].reshape(64, 1),
            "pw_w": c(g["L0_tok_pw_w"].transpose(0, 2, 1)),
            "prm": c(np.stack([g["L0_tok_gamma"], g["L0_tok_beta"], g["L0_tok_pw_b"]], -1)),
            "fc1_w": g["L0_tok_fc1_w"], "fc1_b": g["L0_tok_fc1_b"].reshape(128, 1),
            "fc2_w": g["L0_tok_fc2_w"], "fc2_b": g["L0_tok_fc2_b"].reshape(1, 1),
            **{k: g["L0_attn_" + k] for k in ("Wq", "Wk", "Wv", "Wm", "W1", "W2")},
            **{k: g["L0_attn_" + k].reshape(1, 64) for k in ("g1", "b1", "g2", "b2")},
            "ln_w": g["L0_ffn_ln_w"].reshape(64, 1), "ln_b": g["L0_ffn_ln_b"].reshape(64, 1),
            "ffn_wt": c(g["L0_ffn_W"].T), "ffn_b": g["L0_ffn_b"].reshape(1, 64)}


def kernel(**inputs):
    import numpy as np
    import concourse.bacc as bacc
    from concourse import mybir
    from concourse.bass_utils import run_bass_kernel_spmd as run

    nc = bacc.Bacc("TRN2", target_bir_lowering=False, num_devices=1)
    F32 = mybir.dt.float32
    arrays, t = {}, {}
    for name, a in {**constants(), **laid_out(inputs)}.items():
        arrays[f"in_{name}"] = np.ascontiguousarray(a)
        t[name] = nc.dram_tensor(f"in_{name}", arrays[f"in_{name}"].shape, F32, kind="ExternalInput").ap()
    out = nc.dram_tensor("out_tokens", [B, H + TXT, C], F32, kind="ExternalOutput").ap()
    hcat = nc.dram_tensor("token_scratch", [B, H + TXT, C], F32, kind="Internal").ap()
    build_tokenizer(nc, t, hcat)
    build_mixer(nc, t, hcat, out)
    r = run(nc, [arrays], core_ids=[0])
    return r.results[0]["out_tokens"]
```

```python
import numpy as np

B, H, W, C, LAYERS = 32, 64, 64, 64, 4
MODES = 16
KX, KY = 2 * MODES, MODES
NQ = 8
NK = 8
XP = 768
CH = 1024
HID = 128
TXT = 128
EPS = 1e-5
RSQRT_SEED = 0x5F3759DF


def first(L):
    return isinstance(L, int) and L == 0


def build_tokenizer(nc, t, hcat):
    import concourse.bass as bass
    from concourse import mybir
    from contextlib import ExitStack

    F32, I32, BF16 = mybir.dt.float32, mybir.dt.int32, mybir.dt.bfloat16
    ALU, ACT = mybir.AluOpType, mybir.ActivationFunctionType
    ds = bass.ds
    xparts = nc.dram_tensor("x_parts", [4, 16, 3, 8, XP], BF16, kind="Internal").ap()
    ydram = nc.dram_tensor("y_scratch", [NQ * NK, 128, CH], F32, kind="Internal").ap()

    with ExitStack() as ctx:
        def sb(name, shape, dt=F32):
            return ctx.enter_context(nc.sbuf_tensor(name, shape, dt))

        def sem(name):
            return ctx.enter_context(nc.semaphore(name))

        XY = sb("modes", [128, KX * KY * B])
        WM = sb("mode_weights", [128, 2, 4096])
        ARENA = sb("arena", [128, 16384])
        YC = sb("y_in", [128, 4, CH])
        X1 = sb("row_modes", [128, 4096])
        C1 = sb("c_w_forward", [128, 2, 128])
        C2 = sb("c_h_forward", [128, 2, 128])
        C3 = sb("c_h_inverse", [128, 2, 128])
        C4 = sb("c_w_inverse", [128, 256])
        ID = sb("c_identity", [128, 128])
        AV = sb("c_average", [128, 128])
        PW = sb("pointwise_w", [128, 128])
        FC0 = sb("fc0_w", [128, 128])
        FC0R = sb("fc0_w_rest", [128, 128])
        FC0P = sb("fc0_w_parts", [128, 3, 128], BF16)
        FC0S = sb("fc0_w_stacked", [128, 128], BF16)
        FC0B = sb("fc0_b", [128, 1])
        PRM = sb("layer_params", [128, 3])
        FC1 = sb("fc1_w", [128, 2, HID])
        FC1B = sb("fc1_b", [HID, 1])
        FC2P = sb("fc2_w", [HID, 63])
        FC2B = sb("fc2_b", [32, 1])
        BN = sb("bn_stats", [128, 128, 6])
        MV = sb("bn_small", [128, 16])
        SS = sb("bn_scale_shift", [128, 2])
        XT = [ARENA[:, i * 8192:(i + 1) * 8192] for i in range(2)]
        XC = [ARENA[:, i * 4096:(i + 1) * 4096].rearrange("p (m f b) -> p m f b", f=2, b=B) for i in range(2)]
        YQ = [ARENA[:, i * 2048:(i + 1) * 2048] for i in range(2)]
        T3 = ARENA[:, 4096:6144]
        S4 = [ARENA[:, 8192 + i * 4096:8192 + (i + 1) * 4096] for i in range(2)]
        YO = [X1[:, i * CH:(i + 1) * CH] for i in range(4)]
        G = [ARENA[:, i * CH:(i + 1) * CH] for i in range(4)]
        TO = ARENA[0:32, 8192:8704]
        XS = [XY[:, i * 4 * XP:(i + 1) * 4 * XP] for i in range(2)]
        XPT = XY[:, 8 * XP:14 * XP].bitcast(BF16).rearrange("p (j a c) -> p j a c", j=4, a=3)
        XIN = [WM[:, 1, i * CH:(i + 1) * CH].bitcast(BF16) for i in range(2)]

        PS = [ctx.enter_context(nc.psum_tensor(f"ps{i}", [128, 1024], F32)) for i in range(4)]
        psA, psB = PS[0:2], PS[2:4]
        psT = [PS[0][:, 0:512], PS[0][:, 512:1024]]
        psS = [PS[1][:, 0:512], PS[1][:, 512:1024]]
        psY = PS[2:4]
        ps0 = PS[3]

        s_const = sem("const_loaded")
        s_zero = sem("zeroed")
        s_pwl = sem("pointwise_w_loaded")
        s_prm = sem("params_loaded")
        s_yl = [sem(f"chunk_loaded{i}") for i in range(4)]
        s_xl = [sem(f"image_quarter_loaded{i}") for i in range(4)]
        s_xp = sem("image_split")
        s_xs = [sem(f"image_parts_stored{i}") for i in range(4)]
        s_fw = sem("fc0_w_split")
        s_xin = [sem(f"image_parts_loaded{i}") for i in range(2)]
        s_f0 = sem("fc0_done")
        F0_CREDIT = 4
        s_pst = [sem(f"h0_stored{i}") for i in range(4)]
        s_hc = sem("chunk_activated")
        HC_CREDIT = 1
        s_xt = sem("chunk_transposed")
        XT_CREDIT = 4
        s_s1 = sem("w_transform_done")
        S1_CREDIT = 8
        s_s1e = sem("w_transform_read")
        S1E_CREDIT = 2
        s_s2 = sem("h_transform_done")
        S2_CREDIT = 2
        s_s2e = sem("h_transform_read")
        S2E_CREDIT = 8
        s_wl = [[sem(f"mode_w_loaded{i}{u}") for u in range(2)] for i in range(2)]
        s_xa = sem("form_a_ready")
        s_xlo = sem("form_b_low_ready")
        s_xhi = sem("form_b_high_ready")
        s_mx = sem("mode_products_done")
        MX_CREDIT = 4
        s_mxe = sem("mode_products_read")
        MXE_CREDIT = 4
        s_yq = sem("quad_modes_staged")
        s_t3 = sem("mode_transpose_done")
        T3_CREDIT = 8
        s_t3e = sem("mode_transpose_read")
        T3E_CREDIT = 2
        s_s3 = sem("h_inverse_done")
        S3_CREDIT = 1
        s_s3e = sem("h_inverse_transposed")
        S3E_CREDIT = 2
        s_y = sem("y_done")
        Y_CREDIT = 16
        s_ye = sem("y_read")
        YE_CREDIT = 2
        s_bn = sem("bn_stats_done")
        BN_CREDIT = 4
        s_st = [sem(f"chunk_stored{i}") for i in range(4)]
        ST_CREDIT = 16
        s_sm = sem("bn_small_step")
        s_av = sem("bn_average_done")
        s_ss = sem("scale_shift_ready")
        s_f1 = sem("hidden_done")
        s_f1e = sem("hidden_activated")
        F1E_CREDIT = 2
        s_f2 = sem("head_unit_done")
        F2_CREDIT = 4
        s_to = sem("head_read")
        TO_CREDIT = 2
        s_ts = sem("tokens_stored")
        TS_CREDIT = 128
        s_txt = sem("text_copied")

        block = ctx.enter_context(nc.Block())
        NCONST = 31
        SMALL = 22

        def loaded(L, phase, q, k):
            return 16 * (L * 32 + (phase - 1) * 16 + q * 2 + k // 4 + 1)

        def s2_bank(L, g):
            return psB[0 if first(L) else g]

        @block.sync
        def _(eng):
            for s in s_st:
                eng.nop().then_inc(s, ST_CREDIT)
            eng.nop().then_inc(s_ts, TS_CREDIT)
            for j in range(4):
                eng.dma_start(XS[0][:, j * XP:(j + 1) * XP], t["x"][j]).then_inc(s_xl[j], 16)
            for dst, src in ((C1[:, :, :], t["c1"]), (C2[:, :, :], t["c2"]), (C3[:, :, :], t["c3"]),
                             (C4[:, :], t["c4"]), (ID[:, :], t["ident"]), (AV[:, :], t["avg"]),
                             (FC0B[0:64, :], t["fc0_b"]), (FC0B[64:128, :], t["fc0_b"]),
                             (FC1B[:, :], t["fc1_b"]), (FC2B[:, :], t["fc2_b"].broadcast_to((32, 1)))):
                eng.dma_start(dst, src).then_inc(s_const, 16)
            eng.wait_ge(s_zero, 5)
            for bp in range(2):
                for copy in range(9):
                    r = 32 * (copy // 3) + 6 * (copy % 3) + 3 * bp
                    eng.dma_start(FC0[r:r + 3, 64 * bp:64 * bp + 64], t["fc0_w"]).then_inc(s_const, 16)
                eng.dma_start(FC1[64 * bp:64 * bp + 64, bp, :], t["fc1_w"]).then_inc(s_const, 16)
            eng.dma_start(FC2P[:, 31:32], t["fc2_w"]).then_inc(s_const, 16)
            for j in range(4):
                eng.wait_ge(s_xp, 4 * j + 4)
                for a in range(3):
                    eng.dma_start(xparts[j, :, a], XPT[:, j, a, :]).then_inc(s_xs[j], 16)
            xchunks = xparts.rearrange("j m a e c -> (j m a e c)").rearrange("(n r c) -> n r c", r=18, c=CH)

            def images(quads):
                with quads as q:
                    for m in range(4):
                        eng.wait_ge(s_f0, q * NK + 2 * m + 2)
                        for a in range(3):
                            eng.dma_start(XIN[m % 2][32 * a:32 * a + 18, :].rearrange("r (n c) -> r n c", n=2),
                                          xchunks[ds(q * NK + 2 * m, 2)].rearrange("n r c -> r n c"))\
                               .then_inc(s_xin[m % 2], 16)

            def load(q, k):
                eng.dma_start(YC[:, k % 4, :], ydram[q * NK + k]).then_inc(s_yl[k % 4], 16)

            def passes(free, base, per, store=None, between=None):
                if between is None:
                    for k in range(4):
                        load(0, k)

                def quad(q, last):
                    for k in range(NK):
                        if not (last and k >= 4):
                            eng.wait_ge(free, base + per * (q * NK + k + 1))
                            load(q + (k + 4) // NK, (k + 4) % NK)
                        if store is not None:
                            store(q, k)

                with eng.Fori(0, NQ - 1 if between is None else NQ - 3) as q:
                    quad(q, False)
                if between is not None:
                    for n in range(2):
                        between(n)
                        quad(NQ - 3 + n, False)
                quad(NQ - 1, True)

            def next_pass(L):
                for k in range(4):
                    eng.wait_ge(s_y, Y_CREDIT + L * 64 - 3 + k)
                    eng.wait_ge(s_st[k], ST_CREDIT + L * 256 - 240)
                    load(0, k)

            def mode_weights(L, c):
                for u in range(2):
                    eng.wait_ge(s_mx, L * 16 + 2 * c + u + 1)
                    eng.dma_start(WM[:, c % 2, u * 2048:(u + 1) * 2048],
                                  t["modew"][L * 8 + c, :, u * 2048:(u + 1) * 2048]).then_inc(s_wl[c % 2][u], 16)

            def layer(L):
                def weights(n):
                    if n == 1:
                        if first(L):
                            eng.wait_ge(s_f0, F0_CREDIT + 64)
                        return mode_weights(L, 1)
                    if not first(L):
                        for k in range(4):
                            eng.wait_ge(s_st[k], ST_CREDIT + L * 256)
                        eng.wait_ge(s_ss, L)
                    for bp in range(2):
                        eng.dma_start(PW[64 * bp:64 * bp + 64, 64 * bp:64 * bp + 64], t["pw_w"][L]).then_inc(s_pwl, 16)
                        eng.dma_start(PRM[64 * bp:64 * bp + 64, :], t["prm"][L]).then_inc(s_prm, 16)
                    mode_weights(L, 0)

                if first(L):
                    eng.wait_ge(s_xs[0], 48)
                    images(eng.Fori(0, 2))
                    for j in range(1, 4):
                        eng.wait_ge(s_xs[j], 48)
                    images(eng.Fori(2, NQ))
                    weights(0)
                    weights(1)
                    for k in range(4):
                        eng.wait_ge(s_pst[k], ST_CREDIT + 16 * 16)
                else:
                    next_pass(L)
                    passes(s_xt, XT_CREDIT + L * 64, 1, between=weights)
                for c in range(2, 8):
                    mode_weights(L, c)
                eng.wait_ge(s_xt, XT_CREDIT + L * 64 + 64)

                def store(q, k):
                    eng.wait_ge(s_ye, YE_CREDIT + L * 64 + q * NK + k + 1)
                    eng.dma_start(ydram[q * NK + k], YO[k % 4]).then_inc(s_st[k % 4], 16)

                passes(s_y, Y_CREDIT + L * 64, 1, store)

            layer(0)
            with eng.Fori(1, LAYERS) as L:
                layer(L)
            next_pass(LAYERS)
            hv = hcat.rearrange("(q z bp) s w -> q z bp s w", z=2, bp=2)

            def store_tokens(q, k):
                if k < NK - 1:
                    return
                eng.wait_ge(s_to, TO_CREDIT + q + 1)
                for bp in range(2):
                    for z in range(2):
                        for hh in range(2):
                            src = TO[bp * 16:bp * 16 + 16, :]\
                                .rearrange("r (h z hh w) -> r h z hh w", h=2, z=2, hh=2)[:, :, z, hh, :]
                            dst = hv[q, z, bp, hh * 32:hh * 32 + 32, :].rearrange("(r h) w -> r h w", h=2)
                            eng.dma_start(dst, src).then_inc(s_ts, 16)


            def last_stored(n):
                for k in range(4):
                    eng.wait_ge(s_st[k], ST_CREDIT + LAYERS * 256)

            passes(s_f1, 0, 2, store_tokens, between=last_stored)
            eng.wait_ge(s_ts, TS_CREDIT + NQ * 128)

        @block.gpsimd
        def _(eng):
            eng.memset(PW[:, :], 0.0).then_inc(s_zero, 1)
            eng.memset(FC0[:, :], 0.0).then_inc(s_zero, 1)
            eng.memset(FC1[:, :, :], 0.0).then_inc(s_zero, 1)
            eng.memset(FC2P[:, :], 0.0).then_inc(s_zero, 1)
            eng.memset(WM[:, 1, 0:2 * CH], 0.0).then_inc(s_zero, 1)
            eng.dma_start(hcat[:, H:H + TXT, :], t["txt"]).then_inc(s_txt, 16)
            eng.wait_ge(s_txt, 16)

        @block.tensor
        def _(pe):
            for s, credit in ((s_f0, F0_CREDIT), (s_s1, S1_CREDIT), (s_s2, S2_CREDIT), (s_mx, MX_CREDIT),
                              (s_t3, T3_CREDIT), (s_s3, S3_CREDIT), (s_y, Y_CREDIT), (s_f2, F2_CREDIT)):
                pe.nop().then_inc(s, credit)
            pe.wait_ge(s_const, 16 * NCONST)
            pe.wait_ge(s_fw, 8)

            def fc0(q, k):
                pe.wait_ge(s_xin[k // 2 % 2], 48 * (q * 2 + k // 4 + 1))
                pe.wait_ge(s_hc, HC_CREDIT + q * NK + k)
                for half in range(2):
                    at = (k % 2) * CH + half * 512
                    last = pe.matmul(ps0[:, half * 512:half * 512 + 512], FC0S[:, :],
                                     XIN[k // 2 % 2][:, at:at + 512], start=True, stop=True)
                last.then_inc(s_f0, 1)

            xts = [x.rearrange("p (r wh c) -> p r wh c", wh=2, c=32) for x in XT]
            x1s = X1[:, :].rearrange("p (m k) -> p m k", k=32)
            t3s = T3.rearrange("p (z kk o) -> p o z kk", z=2, kk=16)
            s4s = [x.rearrange("p (m r) -> p m r", r=32) for x in S4]

            def forward(L, q, i, images=False):
                pe.wait_ge(s_xt, XT_CREDIT + L * 64 + (q + 1) * NK)
                for g in range(4):
                    pe.wait_ge(s_s1e, (L * NQ + q) * 4 + g + 1)
                    for cc in range(8):
                        if images and cc % 4 == 0:
                            fc0(q + 1, 2 * g + cc // 4)
                        for wh in range(2):
                            last = pe.matmul(psA[g % 2][:, cc * 128:cc * 128 + 128], xts[i][:, :, wh, g * 8 + cc],
                                             C1[:, wh, :], start=(wh == 0), stop=(wh == 1))
                    last.then_inc(s_s1, 1)
                pe.wait_ge(s_s1e, S1E_CREDIT + (L * NQ + q + 1) * 4)
                for g in range(2):
                    pe.wait_ge(s_s2e, (L * NQ + q) * 8 + g * 4 + 4 + (4 if first(L) else 0))
                    for j in range(8):
                        for ri in range(2):
                            last = pe.matmul(s2_bank(L, g)[:, j * 128:j * 128 + 128], x1s[:, :, ri * KY + g * 8 + j],
                                             C2[:, ri, :], start=(ri == 0), stop=(ri == 1))
                    last.then_inc(s_s2, 1)

            def modes(L, c, i, first):
                for u in range(2):
                    pe.wait_ge(s_wl[i][u], 16 * (L * 4 + first + 1))
                    pe.wait_ge(s_xa, L * 16 + c * 2 + u + 1)
                    pe.wait_ge(s_xlo, L * 16 + c * 2 + u + 1)
                    pe.wait_ge(s_xhi, L * 16 + c * 2 + u + 1)
                    pe.wait_ge(s_mxe, L * 16 + c * 2 + u + 1)
                    for kyh in range(2):
                        for x in range(2):
                            for kyp in range(8):
                                m = (u * 2 + x) * KY + kyh * 8 + kyp
                                at = x * 512 + kyp * 64
                                last = pe.matmul(PS[i * 2 + u][kyh * 64:kyh * 64 + 64, at:at + 64],
                                                 WM[:, i, m * 64:m * 64 + 64],
                                                 XC[i][:, m, :, :].rearrange("p f b -> p (f b)"), start=True, stop=True)
                    last.then_inc(s_mx, 1)

            def turn(L, q, i, g):
                Q = L * NQ + q
                if g == 0:
                    pe.wait_ge(s_yq, (Q + 1) * 2)
                pe.wait_ge(s_t3e, Q * 4 + g + 1)
                for j in range(4):
                    at = ((g % 2) * 4 + j) * 256 + (g // 2) * 128
                    last = pe.transpose(psT[g % 2][:, j * 128:j * 128 + 128], YQ[i][:, at:at + 128], ID[:, :])
                last.then_inc(s_t3, 1)

            def rows(L, q, g):
                Q = L * NQ + q
                if g == 0:
                    pe.wait_ge(s_t3e, T3E_CREDIT + (Q + 1) * 4)
                pe.wait_ge(s_s3e, Q * 8 + g + 1)
                pe.matmul(psS[g % 2], C3[:, g // 4, :], t3s[:, (g % 4) * 16:(g % 4) * 16 + 16, :, :],
                          start=True, stop=True).then_inc(s_s3, 1)

            def sums(L, q, i, k):
                Q = L * NQ + q
                if k == 0:
                    pe.wait_ge(s_s3e, S3E_CREDIT + (Q + 1) * 8)
                pe.wait_ge(s_hc, HC_CREDIT + L * 128 + 64 + q * NK + k + 1)
                pe.wait_ge(s_ye, Q * NK + k + 1)
                for half in range(2):
                    at = half * 512
                    pe.matmul(psY[k % 2][:, at:at + 512], PW[:, :], YC[:, k % 4, at:at + 512], start=True, stop=False)
                    for j in range(2):
                        last = pe.matmul(psY[k % 2][:, at + j * 256:at + j * 256 + 256],
                                         s4s[i][:, :, k * 4 + half * 2 + j], C4[:, :], start=False, stop=(j == 1))
                last.then_inc(s_y, 1)

            def inverse(L, q, i, prepare, finish):
                for k in range(NK):
                    if finish:
                        sums(L, q - 1, 1 - i, k)
                    if prepare and k < 4:
                        turn(L, q, i, k)
                    if prepare and k >= 4:
                        rows(L, q, (k - 4) * 2)
                        rows(L, q, (k - 4) * 2 + 1)

            def layer(L):
                if first(L):
                    for k in range(NK):
                        fc0(0, k)
                    with pe.Fori(0, 3) as h:
                        for i in range(2):
                            forward(L, h * 2 + i, i, images=True)
                    forward(L, 6, 0, images=True)
                    forward(L, 7, 1)
                else:
                    with pe.Fori(0, 4) as h:
                        for i in range(2):
                            forward(L, h * 2 + i, i)
                with pe.Fori(0, 4) as h:
                    for i in range(2):
                        modes(L, h * 2 + i, i, h)
                pe.wait_ge(s_pwl, 32 * (L + 1))
                inverse(L, 0, 0, True, False)
                with pe.Fori(0, 3) as h:
                    inverse(L, h * 2 + 1, 1, True, True)
                    inverse(L, h * 2 + 2, 0, True, True)
                inverse(L, 7, 1, True, True)
                inverse(L, 8, 0, False, True)
                pe.wait_ge(s_sm, L * SMALL + 1)
                pe.matmul(psT[0][:, 0:1], AV[:, :], MV[:, 0:1], start=True, stop=True).then_inc(s_av, 1)
                pe.wait_ge(s_sm, L * SMALL + 4)
                pe.matmul(psT[0][:, 1:2], AV[:, :], MV[:, 4:5], start=True, stop=True).then_inc(s_av, 1)

            layer(0)
            with pe.Fori(1, LAYERS) as L:
                layer(L)

            def head2(q, i, k):
                for bp in range(2):
                    n = q * 16 + k * 2 + bp
                    pe.wait_ge(s_f1e, F1E_CREDIT + n + 1)
                    for half in range(2):
                        r = bp * 16 + k * 2 + half
                        last = pe.matmul(psB[i][0:32, 0:512], FC2P[:, 31 - r:63 - r],
                                         G[(k % 2) * 2 + bp][:, half * 512:half * 512 + 512],
                                         start=(k == 0 and r == 0), stop=(k == NK - 1 and r == 31))
                    last.then_inc(s_f2, 1)

            with pe.Fori(0, 4) as h:
                for i in range(2):
                    q = h * 2 + i
                    pe.wait_ge(s_to, q + 1)
                    for k in range(NK):
                        pe.wait_ge(s_hc, HC_CREDIT + LAYERS * 128 + q * NK + k + 1)
                        for bp in range(2):
                            pe.wait_ge(s_f1e, q * 16 + k * 2 + bp + 1)
                            for half in range(2):
                                last = pe.matmul(psA[bp][:, half * 512:half * 512 + 512], FC1[:, bp, :],
                                                 YC[:, k % 4, half * 512:half * 512 + 512], start=True, stop=True)
                            last.then_inc(s_f1, 1)
                        if k > 0:
                            head2(q, i, k - 1)
                    head2(q, i, NK - 1)

        @block.scalar
        def _(act):
            for s, credit in ((s_hc, HC_CREDIT), (s_s1e, S1E_CREDIT), (s_mxe, MXE_CREDIT), (s_t3e, T3E_CREDIT),
                              (s_ye, YE_CREDIT), (s_f1e, F1E_CREDIT)):
                act.nop().then_inc(s, credit)
            for s in s_pst:
                act.nop().then_inc(s, ST_CREDIT)
            act.wait_ge(s_const, 16 * NCONST)
            x1o = X1[:, :].rearrange("p (cb c k) -> p c cb k", cb=4, c=32)
            xyb = XY[:, :].rearrange("p (m b) -> p m b", b=B)

            def activate(L, phase, q, k):
                if first(L) and phase == 0:
                    n = q * NK + k
                    act.wait_ge(s_f0, F0_CREDIT + n + 1)
                    act.wait_ge(s_pst[k % 4], 16 * (q * 2 + k // 4) + 16)
                    act.wait_ge(s_xt, XT_CREDIT + n - 3)
                    act.activation(YC[:, k % 4, :], ps0[:, :], ACT.Identity, bias=FC0B[:, 0:1]).then_inc(s_hc, 1)
                    act.wait_ge(s_hc, HC_CREDIT + n + 1)
                    act.dma_start(ydram[n], YC[:, k % 4, :]).then_inc(s_pst[k % 4], 16)
                    return
                act.wait_ge(s_yl[k % 4], loaded(L, phase, q, k))
                if first(L):
                    act.nop().then_inc(s_hc, 1)
                else:
                    act.activation(YC[:, k % 4, :], YC[:, k % 4, :], ACT.Gelu, bias=SS[:, 1:2],
                                   scale=SS[:, 0:1]).then_inc(s_hc, 1)

            def read_s1(L, q, ahead=False):
                for g in range(4):
                    if ahead:
                        activate(L, 0, q + 1, 2 * g)
                        activate(L, 0, q + 1, 2 * g + 1)
                    act.wait_ge(s_s1, S1_CREDIT + (L * NQ + q) * 4 + g + 1)
                    if g == 0:
                        act.wait_ge(s_s2, (L * NQ + q) * 2 + 2)
                    act.activation(x1o[:, g * 8:g * 8 + 8, :, :],
                                   psA[g % 2][:, :].rearrange("p (c cb k) -> p c cb k", c=8, cb=4),
                                   ACT.Copy).then_inc(s_s1e, 1)

            def high(L, c, i, u):
                act.wait_ge(s_mx, L * 16 + c * 2 + u + 1)
                act.activation(XC[i][64:128, u * 32:u * 32 + 32, 1, :], xyb[0:64, ds(c * 64 + u * 32, 32), :],
                               ACT.Copy).then_inc(s_xhi, 1)

            def read_modes(L, c, i, u):
                act.wait_ge(s_mx, MX_CREDIT + L * 16 + c * 2 + u + 1)
                act.activation(XY[:, ds(c * 2048 + u * 1024, 1024)], PS[i * 2 + u][:, :], ACT.Copy).then_inc(s_mxe, 1)

            def read_turned(L, q, g):
                Q = L * NQ + q
                act.wait_ge(s_t3, T3_CREDIT + Q * 4 + g + 1)
                if g == 0:
                    act.wait_ge(s_s3, Q * 8 + 1)
                act.activation(T3[:, g * 512:g * 512 + 512], psT[g % 2], ACT.Copy).then_inc(s_t3e, 1)

            def read_sum(L, q, k):
                n = L * 64 + q * NK + k
                act.wait_ge(s_y, Y_CREDIT + n + 1)
                act.wait_ge(s_st[k % 4], 16 * (L * 16 + q * 2 + k // 4) + 16)
                act.wait_ge(s_bn, n + 1)
                act.activation(YO[k % 4], psY[k % 2][:, :], ACT.Identity, bias=PRM[:, 2:3]).then_inc(s_ye, 1)

            def inverse(L, q, prepare, finish, ends):
                for k in range(NK):
                    if finish and not (ends and k == NK - 1):
                        activate(L, 1, q - 1 + (k + 1) // NK, (k + 1) % NK)
                    if finish:
                        read_sum(L, q - 1, k)
                    if prepare and k < 4:
                        read_turned(L, q, k)

            def layer(L):
                if not first(L):
                    act.wait_ge(s_ss, L)
                for k in range(NK):
                    activate(L, 0, 0, k)
                if not first(L):
                    for k in range(4):
                        act.wait_ge(s_st[k], ST_CREDIT + L * 256)
                with act.Fori(0, NQ - 1) as q:
                    read_s1(L, q, ahead=True)
                read_s1(L, NQ - 1)
                act.wait_ge(s_s2e, S2E_CREDIT + L * 64 + 64)
                for i in range(2):
                    for u in range(2):
                        high(L, i, i, u)
                with act.Fori(0, 3) as h:
                    for i in range(2):
                        for u in range(2):
                            high(L, h * 2 + i + 2, i, u)
                            read_modes(L, h * 2 + i, i, u)
                for i in range(2):
                    for u in range(2):
                        read_modes(L, 6 + i, i, u)
                act.wait_ge(s_prm, 32 * (L + 1))
                inverse(L, 0, True, False, False)
                activate(L, 1, 0, 0)
                with act.Fori(1, NQ) as q:
                    inverse(L, q, True, True, False)
                inverse(L, NQ, False, True, True)

            layer(0)
            with act.Fori(1, LAYERS) as L:
                layer(L)

            def hidden(q, k):
                for bp in range(2):
                    n = q * 16 + k * 2 + bp
                    act.wait_ge(s_f1, n + 1)
                    act.wait_ge(s_f2, n + 1)
                    act.activation(G[(k % 2) * 2 + bp], psA[bp][:, :], ACT.Gelu, bias=FC1B[:, 0:1]).then_inc(s_f1e, 1)

            act.wait_ge(s_ss, LAYERS)
            activate(LAYERS, 0, 0, 0)
            with act.Fori(0, NQ - 1) as q:
                for k in range(NK):
                    activate(LAYERS, 0, q + (k + 1) // NK, (k + 1) % NK)
                    hidden(q, k)
            for k in range(NK):
                if k < NK - 1:
                    activate(LAYERS, 0, NQ - 1, k + 1)
                hidden(NQ - 1, k)

        @block.vector
        def _(dve):
            for s, credit in ((s_xt, XT_CREDIT), (s_s2e, S2E_CREDIT), (s_s3e, S3E_CREDIT), (s_bn, BN_CREDIT), (s_to, TO_CREDIT)):
                dve.nop().then_inc(s, credit)
            def split(x, rest, parts, done, base):
                def do(instruction, n):
                    instruction.then_inc(done, 1)
                    if n < 4:
                        dve.wait_ge(done, base + n)

                do(dve.tensor_copy(parts[0], x), 1)
                do(dve.tensor_tensor(rest, x, parts[0], ALU.subtract), 2)
                do(dve.tensor_copy(parts[1], rest), 3)
                do(dve.tensor_tensor(parts[2], rest, parts[1], ALU.subtract), 4)

            for j in range(4):
                dve.wait_ge(s_xl[j], 16)
                x, rest = (s[:, j * XP:(j + 1) * XP] for s in XS)
                split(x, rest, [XPT[:, j, a, :] for a in range(3)], s_xp, 4 * j)
            dve.wait_ge(s_const, 16 * NCONST)
            split(FC0[:, :], FC0R[:, :], [FC0P[:, a, :] for a in range(3)], s_fw, 0)
            dve.wait_ge(s_fw, 4)
            dve.memset(FC0S[:, :], 0.0).then_inc(s_fw, 1)
            dve.wait_ge(s_fw, 5)
            for a in range(3):
                dve.tensor_copy(FC0S[32 * a:32 * a + 32, :], FC0P[32 * a:32 * a + 32, a, :]).then_inc(s_fw, 1)
            xo = XY[:, :].rearrange("p (kx ky q z bp) -> p q bp ky z kx", kx=KX, ky=KY, q=NQ, z=2)
            xyb = XY[:, :].rearrange("p (m b) -> p m b", b=B)

            def transposes(L, q, i):
                for k in range(NK):
                    dve.wait_ge(s_hc, HC_CREDIT + L * 128 + q * NK + k + 1)
                    if k == 0:
                        dve.wait_ge(s_s1, (L * NQ + q) * 4 + 4)
                    dve.transpose(XT[i][:, k * CH:k * CH + CH], YC[:, k % 4, :]).then_inc(s_xt, 1)

            def read_s2(L, q):
                for g in range(2):
                    dve.wait_ge(s_s2, S2_CREDIT + (L * NQ + q) * 2 + g + 1)
                    for bp in range(2):
                        src = s2_bank(L, g)[bp * 64:bp * 64 + 64, :].rearrange("p (ky ri z kx) -> p ri ky z kx", ky=8, ri=2, z=2)
                        for ri in range(2):
                            dve.tensor_copy(xo[ri * 64:ri * 64 + 64, q, bp, g * 8:g * 8 + 8, :, :],
                                            src[:, ri, :, :, :]).then_inc(s_s2e, 1)

            def forms(L, c, i):
                for u in range(2):
                    m = ds(c * 64 + u * 32, 32)
                    dve.wait_ge(s_s2e, S2E_CREDIT + L * 64 + 64)
                    dve.wait_ge(s_mx, L * 16 + c * 2 + u + 1)
                    dve.tensor_copy(XC[i][:, u * 32:u * 32 + 32, 0, :], xyb[:, m, :]).then_inc(s_xa, 1)
                    dve.tensor_scalar(XC[i][0:64, u * 32:u * 32 + 32, 1, :], xyb[64:128, m, :], -1.0, None,
                                      ALU.mult).then_inc(s_xlo, 1)

            yv = XY[:, :].rearrange("p (kx kyp ri b) -> p kyp b kx ri", kx=KX, kyp=8, ri=2)
            yqv = [y.rearrange("p (kyp b kx ri) -> p kyp b kx ri", kyp=8, b=4, kx=KX) for y in YQ]

            def stage(L, q, i):
                dve.wait_ge(s_mxe, MXE_CREDIT + L * 16 + 16)
                dve.wait_ge(s_t3, (L * NQ + q) * 4 + 4)
                for ri in range(2):
                    dve.tensor_copy(yqv[i][:, :, :, :, ri], yv[:, :, ds(q * 4, 4), :, ri]).then_inc(s_yq, 1)

            def read_rows(L, q, i, g):
                Q = L * NQ + q
                dve.wait_ge(s_s3, S3_CREDIT + Q * 8 + g + 1)
                if g == 0:
                    dve.wait_ge(s_y, Q * 8 + 8)
                dve.transpose(S4[i][:, g * 512:g * 512 + 512], psS[g % 2]).then_inc(s_s3e, 1)

            def stats(L, q, k):
                n = L * 64 + q * NK + k
                dve.wait_ge(s_ye, YE_CREDIT + n + 1)
                dve.bn_stats(BN[:, ds(q * 16 + k * 2, 1), :].rearrange("p a s -> p (a s)"), YO[k % 4][:, 0:512])
                dve.bn_stats(BN[:, ds(q * 16 + k * 2 + 1, 1), :].rearrange("p a s -> p (a s)"),
                             YO[k % 4][:, 512:1024]).then_inc(s_bn, 1)

            def inverse(L, q, i, prepare, finish, following=True):
                for k in range(NK):
                    if finish:
                        stats(L, q - 1, k)
                    if k == 2 and prepare and following:
                        stage(L, q + 1, 1 - i)
                    if prepare and k >= 4:
                        read_rows(L, q, i, (k - 4) * 2)
                        read_rows(L, q, i, (k - 4) * 2 + 1)

            def scale_shift(L):
                base = L * SMALL
                steps = [0]

                def step(instruction):
                    instruction.then_inc(s_sm, 1)
                    steps[0] += 1
                    dve.wait_ge(s_sm, base + steps[0])

                def col(i):
                    return MV[:, i:i + 1]

                dve.wait_ge(s_bn, BN_CREDIT + L * 64 + 64)
                dve.memset(MV[:, 15:16], 0.0)
                step(dve.bn_aggr(MV[:, 0:2], BN[:, :, :].rearrange("p n s -> p (n s)")))
                dve.wait_ge(s_av, 2 * L + 1)
                step(dve.tensor_copy(col(2), psT[0][:, 0:1]))
                step(dve.tensor_tensor(col(3), col(0), col(2), ALU.subtract))
                step(dve.scalar_tensor_tensor(out=col(4), in0=col(3), scalar=col(3), in1=col(1),
                                              op0=ALU.mult, op1=ALU.add))
                dve.wait_ge(s_av, 2 * L + 2)
                step(dve.tensor_scalar(col(5), psT[0][:, 1:2], EPS, None, ALU.add))
                step(dve.tensor_scalar(col(6).bitcast(I32), col(5).bitcast(I32), 1, None, ALU.logical_shift_right))
                step(dve.tensor_scalar(col(6).bitcast(I32), col(6).bitcast(I32), -1, RSQRT_SEED, ALU.mult, ALU.add))
                for _ in range(4):
                    step(dve.scalar_tensor_tensor(out=col(7), in0=col(6), scalar=-0.5, in1=col(6),
                                                  op0=ALU.mult, op1=ALU.mult))
                    step(dve.tensor_tensor(col(7), col(7), col(5), ALU.mult))
                    step(dve.scalar_tensor_tensor(out=col(6), in0=col(7), scalar=1.5, in1=col(6),
                                                  op0=ALU.add, op1=ALU.mult))
                dve.wait_ge(s_prm, 32 * (L + 1))
                step(dve.tensor_tensor(SS[:, 0:1], col(6), PRM[:, 0:1], ALU.mult))
                step(dve.tensor_tensor(col(8), col(2), SS[:, 0:1], ALU.mult))
                step(dve.tensor_tensor(SS[:, 1:2], PRM[:, 1:2], col(8), ALU.subtract))
                assert steps[0] == SMALL
                dve.nop().then_inc(s_ss, 1)

            def layer(L):
                transposes(L, 0, 0)
                if first(L):
                    for j in range(4):
                        dve.wait_ge(s_xs[j], 48)
                with dve.Fori(0, 3) as h:
                    for i in range(2):
                        transposes(L, h * 2 + i + 1, 1 - i)
                        read_s2(L, h * 2 + i)
                transposes(L, 7, 1)
                read_s2(L, 6)
                read_s2(L, 7)
                with dve.Fori(0, 4) as h:
                    for i in range(2):
                        forms(L, h * 2 + i, i)
                stage(L, 0, 0)
                inverse(L, 0, 0, True, False)
                with dve.Fori(0, 3) as h:
                    inverse(L, h * 2 + 1, 1, True, True)
                    inverse(L, h * 2 + 2, 0, True, True)
                inverse(L, 7, 1, True, True, following=False)
                inverse(L, 8, 0, False, True)
                scale_shift(L)

            layer(0)
            with dve.Fori(1, LAYERS) as L:
                layer(L)
            dve.wait_ge(s_const, 16 * NCONST)
            with dve.Fori(0, 4) as h:
                for i in range(2):
                    q = h * 2 + i
                    dve.wait_ge(s_f2, F2_CREDIT + (q + 1) * 16)
                    dve.wait_ge(s_ts, 128 * q + TS_CREDIT)
                    dve.tensor_scalar(TO, psB[i][0:32, 0:512], FC2B[:, 0:1], None, ALU.add).then_inc(s_to, 1)


def build_mixer(nc, t, hcat, out):
    import concourse.bass as bass
    from concourse import mybir
    from contextlib import ExitStack

    F32, I32 = mybir.dt.float32, mybir.dt.int32
    ALU, ACT, AX = mybir.AluOpType, mybir.ActivationFunctionType, mybir.AxisListType
    L = H + TXT
    NT = B * L // 128
    NP = NT // 2
    NG = 6
    ITERS = 30
    ATT_EPS = 1e-6

    with ExitStack() as ctx:
        def sb(name, shape, dt=F32):
            return ctx.enter_context(nc.sbuf_tensor(name, shape, dt))

        def sem(name):
            return ctx.enter_context(nc.semaphore(name))

        HT = sb("tokens", [128, NT, C])
        XN = sb("tokens_normed", [128, NT, C])
        XNT = sb("tokens_normed_t", [128, NP, 128])
        QT = sb("queries_t", [128, NP, 128])
        KE = sb("keys", [128, NT, C])
        VE = sb("values", [128, NT, C + 1])
        VH = sb("values_halved", [128, 2, NT // 3, C + 1])
        KVM = sb("key_value", [128, B, 2, 128])
        MS = sb("message", [128, NT, C])
        MT = sb("message_t", [128, NP, 128])
        D = sb("centered", [128, NT, C])
        E = sb("work", [128, NT, C])
        HIDT = sb("hidden_t", [128, 2, NP, 128])
        ST = sb("row_stats", [128, 8, NT])
        WQ = sb("w_q", [128, 128])
        WKV = sb("w_kv", [128, 256])
        WMB = sb("w_m", [128, 128])
        W1X = sb("w_1_x", [128, 2, 128])
        W1M = sb("w_1_m", [128, 2, 128])
        W2 = sb("w_2", [128, C])
        GB = sb("gains", [128, 5, C])
        ID = sb("c_identity2", [128, 128])
        MASK = sb("c_heads", [128, 2, C])
        HALF = sb("c_halves", [128, 2])
        CEN = sb("c_center", [128, 128])
        WF = sb("w_ffn_t", [128, 128])
        LNW = sb("ffn_ln_w", [128, 1])
        LNB = sb("ffn_ln_b", [64, 1])
        LNBR = sb("ffn_ln_b_rows", [64, 128])
        WA = sb("w_ffn_scaled", [128, 128])
        RW = sb("w_ffn_centered", [128, 2, 65])
        MC = sb("c_mean_columns", [128, 2])
        BF = sb("ffn_bias", [128, C])
        PM = ctx.enter_context(nc.psum_tensor("pm", [128, 8 * 512], F32))
        PS = [PM[:, i * 512:i * 512 + 512] for i in range(8)]
        FY = [PM[:, i:i + 1024].rearrange("p (k r) -> p k r", k=2)[:, :, 0:390].rearrange("p k (j c) -> p k j c", c=65)
              for i in (2048, 3072)]

        s_ht = [sem(f"tokens_loaded{g}") for g in range(NG)]
        s_in = sem("mixer_inputs_loaded")
        s_z = sem("mixer_zeroed")
        s_dve = sem("dve_step")
        s_ln = [sem(f"ln{i}_centered") for i in range(4)]
        s_sq = [sem(f"ln{i}_squared") for i in range(4)]
        s_xn = sem("x_normed")
        s_xt = sem("x_turned")
        s_xte = sem("x_turned_read")
        s_kv = sem("kv_done")
        s_kvm = sem("k_clipped")
        s_kx = sem("k_exp_done")
        s_ke = sem("keys_ready")
        s_ve = sem("values_ready")
        s_q = sem("q_done")
        s_qm = sem("q_clipped")
        s_qx = sem("q_exp_done")
        s_qe = sem("queries_ready")
        s_c = sem("contexts_done")
        s_ce = sem("contexts_ready")
        s_m = sem("messages_done")
        s_me = sem("messages_ready")
        s_mt = sem("messages_turned")
        s_mte = sem("messages_turned_read")
        s_p = sem("messages_projected")
        s_pn = sem("messages_normed")
        s_pt = sem("normed_turned")
        s_pte = sem("normed_turned_read")
        s_h = sem("hidden_done2")
        s_he = sem("hidden_read2")
        s_o = sem("w2_done")
        s_wf = sem("ffn_weights")
        s_wfe = sem("ffn_weights_ready")
        s_r = sem("ffn_input_ready")
        s_th = sem("ffn_tanh")
        s_hp = sem("ffn_nudged")
        s_s = sem("ffn_gated")
        s_s2 = sem("ffn_squared")
        s_ft = sem("ffn_turned")
        s_fy = sem("ffn_product")
        s_sc = sem("ffn_scaled")
        s_ms = sem("ffn_mean_squared")
        s_ftr = sem("ffn_turned_read")
        FTE_CREDIT = 4
        FY_CREDIT = 4
        SC_CREDIT = 2
        s_fs = sem("ffn_small_step")
        s_rd = sem("ffn_squares_summed")
        s_v = sem("ffn_variance")
        s_pn2 = sem("w2_normed")
        s_res = sem("residual_added")
        s_fin = sem("result_ready")
        s_out = sem("out_stored")
        NIN = 28
        SMALL2 = 10
        PARTS = 4
        PT = NT // PARTS
        block = ctx.enter_context(nc.Block())

        def grp(x, g):
            return x[:, g * 8:g * 8 + 8, :]

        def bank(g):
            return PS[g][:, :].rearrange("p (t c) -> p t c", c=C)

        def pairs(x, g):
            return x[:, g * 4:g * 4 + 4, :].rearrange("p i t -> p (i t)")

        @block.sync
        def _(eng):
            tokens = hcat.rearrange("b s c -> (b s) c").rearrange("(t p) c -> p t c", p=128)
            for g in range(NG):
                eng.dma_start(grp(HT, g), tokens[:, g * 8:g * 8 + 8, :]).then_inc(s_ht[g], 16)
            eng.wait_ge(s_z, 6)
            for g in range(2):
                a = slice(64 * g, 64 * g + 64)
                for dst, src in ((WQ[a, a], "Wq"), (WKV[a, a], "Wk"), (WKV[a, 128 + 64 * g:192 + 64 * g], "Wv"),
                                 (WMB[a, a], "Wm"), (WF[a, a], "ffn_wt"), (LNW[a, :], "ln_w")):
                    eng.dma_start(dst, t[src]).then_inc(s_in, 16)
                eng.dma_start(W1X[a, g, :], t["W1"][0:64, :]).then_inc(s_in, 16)
                eng.dma_start(W1M[a, g, :], t["W1"][64:128, :]).then_inc(s_in, 16)
            for i, n in enumerate(("g1", "b1", "g2", "b2", "ffn_b")):
                eng.dma_start(GB[:, i, :], t[n].broadcast_to((128, C))).then_inc(s_in, 16)
            for dst, src in ((W2[:, :], t["W2"]), (ID[:, :], t["ident"]), (MASK[:, :, :], t["heads"]), (HALF[:, :], t["halves"]), (CEN[:, :], t["center"]),
                             (MC[:, :], t["meancol"])):
                eng.dma_start(dst, src).then_inc(s_in, 16)
            eng.dma_start(LNB[:, :], t["ln_b"]).then_inc(s_in, 16)
            eng.wait_ge(s_fin, NG)
            eng.dma_start(out.rearrange("b s c -> (b s) c").rearrange("(t p) c -> p t c", p=128), HT[:, :, :]).then_inc(s_out, 16)
            eng.wait_ge(s_out, 16)

        @block.gpsimd
        def _(eng):
            eng.memset(WQ[:, :], 0.0).then_inc(s_z, 1)
            eng.memset(WKV[:, :], 0.0).then_inc(s_z, 1)
            eng.memset(WMB[:, :], 0.0).then_inc(s_z, 1)
            eng.memset(WF[:, :], 0.0).then_inc(s_z, 1)
            eng.memset(W1X[:, :, :], 0.0).then_inc(s_z, 1)
            eng.memset(W1M[:, :, :], 0.0).then_inc(s_z, 1)
            eng.memset(VE[:, :, C:C + 1], 1.0).then_inc(s_z, 1)
            eng.wait_ge(s_xn, 2 * NG)
            eng.wait_ge(s_wfe, 1)
            eng.nop().then_inc(s_r, PARTS)
            bias = BF[:, :].rearrange("p (o c) -> p o c", o=1).broadcast_to((128, PT, C))

            def variance(m, k):
                v = ST[:, 2, k * PT:(k + 1) * PT]
                eng.wait_ge(s_rd, m + 1)
                eng.wait_ge(s_ms, m + 1)
                eng.tensor_tensor(v, ST[:, 1, k * PT:(k + 1) * PT], ST[:, 4, k * PT:(k + 1) * PT], ALU.subtract).then_inc(s_v, 1)

            def biased(m, k):
                eng.wait_ge(s_sc, SC_CREDIT + m + 1)
                x = XN[:, k * PT:(k + 1) * PT, :]
                eng.tensor_tensor(x, x, bias, ALU.add).then_inc(s_r, 1)

            variance(0, 0)
            variance(1, 1)
            with eng.Fori(0, ITERS - 1) as n:
                for k in range(PARTS):
                    biased(PARTS * n + k, k)
                    variance(PARTS * n + k + 2, (k + 2) % PARTS)
            for k in range(PARTS):
                biased(PARTS * (ITERS - 1) + k, k)
                if k < 2:
                    variance(PARTS * (ITERS - 1) + k + 2, k + 2)

        def span(b):
            m, j = b // 2, 3 * (b // 2)
            full, i = (j, 0) if b % 2 == 0 else (j + 2, 1)
            return [(KE[:, full, :], VE[:, full, :]), (KE[:, j + 1, :], VH[:, i, m, :])]

        @block.tensor
        def _(pe):
            pe.wait_ge(s_in, 16 * NIN)
            for g in range(NG):
                pe.wait_ge(s_xn, g + 1)
                if g >= 2:
                    pe.wait_ge(s_xte, g - 1)
                for i in range(4):
                    last = pe.transpose(PS[6 + g % 2][:, i * 128:i * 128 + 128],
                                        XN[:, g * 8 + 2 * i:g * 8 + 2 * i + 2, :].rearrange("p t c -> p (t c)"), ID[:, :])
                last.then_inc(s_xt, 1)
            for u in range(2 * NG):
                if u % 2 == 0:
                    pe.wait_ge(s_xte, u // 2 + 1)
                if u >= 6:
                    pe.wait_ge(s_ke, u - 5)
                    pe.wait_ge(s_ve, u - 5)
                for i in range(2):
                    last = pe.matmul(PS[u % 6][:, i * 256:i * 256 + 256], XNT[:, u * 2 + i, :], WKV[:, :], start=True, stop=True)
                last.then_inc(s_kv, 1)
            for g in range(NG):
                if g >= 2:
                    pe.wait_ge(s_qe, g - 1)
                pe.matmul(PS[6 + g % 2][:, :], WQ[:, :], pairs(XNT, g), start=True, stop=True).then_inc(s_q, 1)
            pe.wait_ge(s_ke, 12)
            pe.wait_ge(s_ve, 14)
            for u in range(B // 4):
                if u >= 6:
                    pe.wait_ge(s_ce, 4 * (u - 5))
                for i in range(4):
                    for half in range(2):
                        for n, (k, v) in enumerate(span(u * 4 + i)):
                            last = pe.matmul(PS[u % 6][half * 64:half * 64 + 64, i * 128:i * 128 + 65],
                                             k, v, start=(n == 0), stop=(n == 1))
                last.then_inc(s_c, 1)
            pe.wait_ge(s_ce, B)
            pe.wait_ge(s_qe, NG)
            for u in range(NT // 4):
                if u >= 6:
                    pe.wait_ge(s_me, u - 5)
                for i in range(4):
                    j = u * 4 + i
                    whole = {0: 2 * (j // 3), 2: 2 * (j // 3) + 1}.get(j % 3)
                    o = PS[u % 6][:, i * 128:i * 128 + 128]
                    if whole is not None:
                        last = pe.matmul(o, QT[:, j // 2, :], KVM[:, whole, j % 2, :], start=True, stop=True)
                    else:
                        for n in range(2):
                            last = pe.matmul(o[n * 64:n * 64 + 64, :], QT[:, j // 2, n * 64:n * 64 + 64],
                                             KVM[:, 2 * (j // 3) + n, j % 2, :], start=True, stop=True)
                last.then_inc(s_m, 1)
            for g in range(NG):
                pe.wait_ge(s_me, 2 * g + 2)
                if g >= 2:
                    pe.wait_ge(s_mte, g - 1)
                for i in range(4):
                    last = pe.transpose(PS[6 + g % 2][:, i * 128:i * 128 + 128],
                                        MS[:, g * 8 + 2 * i:g * 8 + 2 * i + 2, :].rearrange("p t c -> p (t c)"), ID[:, :])
                last.then_inc(s_mt, 1)
            pe.wait_ge(s_me, 12)
            for g in range(NG):
                pe.wait_ge(s_mte, g + 1)
                for i in range(4):
                    last = pe.matmul(PS[g][:, i * 128:i * 128 + 128], MT[:, g * 4 + i, :], WMB[:, :], start=True, stop=True)
                last.then_inc(s_p, 1)
            for g in range(NG):
                pe.wait_ge(s_pn, g + 1)
                if g >= 2:
                    pe.wait_ge(s_pte, g - 1)
                for i in range(4):
                    last = pe.transpose(PS[6 + g % 2][:, i * 128:i * 128 + 128],
                                        MS[:, g * 8 + 2 * i:g * 8 + 2 * i + 2, :].rearrange("p t c -> p (t c)"), ID[:, :])
                last.then_inc(s_pt, 1)
            pe.wait_ge(s_pte, NG)
            for u in range(2 * NG):
                g = u // 2
                if u >= 2:
                    pe.wait_ge(s_he, u - 1)
                pe.matmul(PS[6 + u % 2][:, :], W1X[:, u % 2, :], pairs(XNT, g), start=True, stop=False)
                pe.matmul(PS[6 + u % 2][:, :], W1M[:, u % 2, :], pairs(MT, g), start=False, stop=True).then_inc(s_h, 1)
            for g in range(NG):
                pe.wait_ge(s_he, 2 * g + 2)
                for j in range(8):
                    last = pe.matmul(PS[g][:, j * 64:j * 64 + 64], HIDT[:, j % 2, g * 4 + j // 2, :], W2[:, :], start=True, stop=True)
                last.then_inc(s_o, 1)
            pe.wait_ge(s_wf, 2)
            pe.matmul(PS[6][:, 0:128], CEN[:, :], WA[:, :], start=True, stop=True)
            pe.matmul(PS[7][:, 0:64], LNBR[:, :], WF[0:64, 0:64], start=True, stop=True).then_inc(s_wf, 1)
            pe.wait_ge(s_wfe, 1)

            pe.nop().then_inc(s_fy, FY_CREDIT)
            with pe.Fori(0, ITERS) as n:
                for k in range(PARTS):
                    m = PARTS * n + k
                    pe.wait_ge(s_s, m + 1)
                    pe.wait_ge(s_ftr, 2 * m + FTE_CREDIT)
                    for i in range(6):
                        j = k * PT + 2 * i
                        last = pe.transpose(PS[2 * (k % 2) + i // 3][:, (i % 3) * 128:(i % 3) * 128 + 128],
                                            MS[:, j:j + 2, :].rearrange("p t c -> p (t c)"), ID[:, :])
                        if i % 3 == 2:
                            last.then_inc(s_ft, 1)
                    pe.wait_ge(s_sc, m + SC_CREDIT - 1)
                    for i in range(6):
                        if i % 3 == 0:
                            pe.wait_ge(s_ftr, FTE_CREDIT + 2 * m + i // 3 + 1)
                        last = pe.matmul(PS[4 + 2 * (k % 2) + i // 3][:, (i % 3) * 130:(i % 3) * 130 + 130],
                                         MT[:, k * 6 + i, :], RW[:, :, :].rearrange("p g c -> p (g c)"), start=True, stop=True)
                    last.then_inc(s_fy, 1)

        @block.scalar
        def _(act):
            def squares(n):
                for g in range(NG):
                    act.wait_ge(s_ln[n], g + 1)
                    act.activation(grp(E, g), grp(D, g), ACT.Square).then_inc(s_sq[n], 1)

            squares(0)
            act.wait_ge(s_in, 16 * NIN)
            for g in range(NG):
                act.wait_ge(s_xt, g + 1)
                act.activation(pairs(XNT, g), PS[6 + g % 2][:, :], ACT.Copy).then_inc(s_xte, 1)
            for u in range(2 * NG):
                act.wait_ge(s_kv, u + 1)
                kv = PS[u % 6][:, :].rearrange("p (i k g c) -> p k i g c", i=2, k=2, g=2)
                act.wait_ge(s_z, 7)
                act.activation(VE[:, u * 4:u * 4 + 4, 0:C].rearrange("p (i g) c -> p i g c", g=2), kv[:, 1], ACT.Copy,
                               scale=1.0 / L).then_inc(s_ve, 1)
                act.wait_ge(s_kvm, u + 1)
                act.activation(E[:, u * 4:u * 4 + 4, :], E[:, u * 4:u * 4 + 4, :], ACT.Exp).then_inc(s_kx, 1)
            act.wait_ge(s_ve, 12)
            for i in range(2):
                act.activation(VH[:, i, :, :], VE[:, :, :].rearrange("p (m a) c -> p m a c", a=3)[:, :, 1, :], ACT.Copy,
                               scale=HALF[:, i:i + 1]).then_inc(s_ve, 1)
            for g in range(NG):
                act.wait_ge(s_qm, g + 1)
                act.activation(grp(D, g), grp(D, g), ACT.Exp).then_inc(s_qx, 1)
            for g in range(NG):
                act.wait_ge(s_mt, g + 1)
                act.activation(pairs(MT, g), PS[6 + g % 2][:, :], ACT.Copy).then_inc(s_mte, 1)
            squares(1)
            for g in range(NG):
                act.wait_ge(s_pt, g + 1)
                act.wait_ge(s_p, NG)
                act.activation(pairs(MT, g), PS[6 + g % 2][:, :], ACT.Copy).then_inc(s_pte, 1)
            for u in range(2 * NG):
                act.wait_ge(s_h, u + 1)
                act.activation(HIDT[:, u % 2, (u // 2) * 4:(u // 2) * 4 + 4, :].rearrange("p i t -> p (i t)"),
                               PS[6 + u % 2][:, :], ACT.Relu).then_inc(s_he, 1)
            squares(2)
            squares(3)

            def part(x, k):
                return x[:, k * PT:(k + 1) * PT, :]

            act.nop().then_inc(s_ftr, FTE_CREDIT)
            act.preload_act_table_set("silu_and_others")

            def tanh(m, k):
                act.wait_ge(s_r, m + 1)
                act.activation(part(D, k), part(XN, k), ACT.Tanh).then_inc(s_th, 1)

            def mean_square(m, k):
                act.wait_ge(s_fy, FY_CREDIT + m + 1)
                act.activation(ST[:, 4, k * PT:(k + 1) * PT].rearrange("p (b j) -> p b j", b=2), FY[k % 2][:, :, :, 64],
                               ACT.Square, scale=float(C) ** 0.5).then_inc(s_ms, 1)

            def quarter(m, k, before, after):
                act.wait_ge(s_hp, m + 1)
                act.activation(part(MS, k), part(D, k), ACT.Silu).then_inc(s_s, 1)
                if after:
                    tanh(m + 1, (k + 1) % PARTS)
                if before:
                    mean_square(m - 1, (k - 1) % PARTS)
                act.wait_ge(s_s, m + 1)
                act.wait_ge(s_fy, m + 1)
                for i in range(2):
                    act.wait_ge(s_ft, 2 * m + i + 1)
                    act.activation(MT[:, k * 6 + i * 3:k * 6 + i * 3 + 3, :].rearrange("p i t -> p (i t)"),
                                   PS[2 * (k % 2) + i][:, 0:384], ACT.Copy).then_inc(s_ftr, 1)
                act.activation(part(E, k), part(MS, k), ACT.Square).then_inc(s_s2, 1)

            tanh(0, 0)
            for k in range(PARTS):
                quarter(k, k, k > 0, True)
            with act.Fori(1, ITERS - 1) as n:
                for k in range(PARTS):
                    quarter(PARTS * n + k, k, True, True)
            for k in range(PARTS):
                quarter(PARTS * (ITERS - 1) + k, k, True, k < PARTS - 1)
            mean_square(PARTS * ITERS - 1, PARTS - 1)

        @block.vector
        def _(dve):
            steps = [0]

            def step(instruction):
                instruction.then_inc(s_dve, 1)
                steps[0] += 1
                dve.wait_ge(s_dve, steps[0])

            def spread(x, g):
                return x[:, g * 8:g * 8 + 8].rearrange("p (t o) -> p t o", o=1).broadcast_to((128, 8, C))

            def rsqrt(v, y, w, x, do, g=1.0):
                do(dve.tensor_scalar(y.bitcast(I32), v.bitcast(I32), -0.5, float(RSQRT_SEED), ALU.mult, ALU.add))
                do(dve.tensor_tensor(w, y, y, ALU.mult))
                do(dve.tensor_tensor(w, w, v, ALU.mult))
                do(dve.tensor_scalar(x, w, 0.375 * g, -1.25 * g, ALU.mult, ALU.add))
                do(dve.tensor_tensor(w, w, x, ALU.mult))
                do(dve.scalar_tensor_tensor(out=y, in0=w, scalar=1.875 * g, in1=y, op0=ALU.add, op1=ALU.mult))
                do(dve.scalar_tensor_tensor(out=w, in0=y, scalar=-0.5 / g ** 2, in1=y, op0=ALU.mult, op1=ALU.mult))
                do(dve.tensor_tensor(w, w, v, ALU.mult))
                do(dve.scalar_tensor_tensor(out=y, in0=w, scalar=1.5, in1=y, op0=ALU.add, op1=ALU.mult))

            def norm(n, src, ready, dst, done, gain=None):
                for g in range(NG):
                    if n == 0:
                        dve.wait_ge(s_ht[g], 16)
                    if ready is not None:
                        dve.wait_ge(ready, g + 1)
                    step(dve.tensor_reduce(ST[:, 0, g * 8:g * 8 + 8], src(g), axis=AX.X, op=ALU.add))
                step(dve.tensor_scalar(ST[:, 0, :], ST[:, 0, :], 1.0 / C, None, ALU.mult))
                for g in range(NG):
                    dve.tensor_tensor(grp(D, g), src(g), spread(ST[:, 0, :], g), ALU.subtract).then_inc(s_ln[n], 1)
                for g in range(NG):
                    dve.wait_ge(s_sq[n], g + 1)
                    step(dve.tensor_reduce(ST[:, 1, g * 8:g * 8 + 8], grp(E, g), axis=AX.X, op=ALU.add))
                step(dve.tensor_scalar(ST[:, 2, :], ST[:, 1, :], 1.0 / C, EPS, ALU.mult, ALU.add))
                rsqrt(ST[:, 2, :], ST[:, 3, :], ST[:, 4, :], ST[:, 5, :], step)
                for g in range(NG):
                    r = dve.tensor_tensor(grp(dst, g), grp(D, g), spread(ST[:, 3, :], g), ALU.mult)
                    if gain is not None:
                        step(r)
                        step(dve.tensor_tensor(grp(dst, g), grp(dst, g), GB[:, gain:gain + 1, :].broadcast_to((128, 8, C)), ALU.mult))
                        r = dve.tensor_tensor(grp(dst, g), grp(dst, g), GB[:, gain + 1:gain + 2, :].broadcast_to((128, 8, C)), ALU.add)
                    r.then_inc(done, 1)

            norm(0, lambda g: grp(HT, g), None, XN, s_xn)
            dve.wait_ge(s_in, 16 * NIN)
            dve.wait_ge(s_xn, NG)
            def key_clip(u):
                kv = PS[u % 6][:, :].rearrange("p (i k g c) -> p k i g c", i=2, k=2, g=2)
                dve.wait_ge(s_kv, u + 1)
                dve.wait_ge(s_ve, u + 1)
                dve.tensor_scalar(E[:, u * 4:u * 4 + 4, :].rearrange("p (i g) c -> p i g c", g=2), kv[:, 0], 0.0, None,
                                  ALU.min).then_inc(s_kvm, 1)

            def key_sum(u):
                kv = PS[u % 6][:, :].rearrange("p (i k gc) -> p k i gc", i=2, k=2)
                dve.wait_ge(s_kx, u + 1)
                dve.scalar_tensor_tensor(out=KE[:, u * 4:u * 4 + 4, :].rearrange("p (i g) c -> p i (g c)", g=2), in0=kv[:, 0],
                                         scalar=0.0, in1=E[:, u * 4:u * 4 + 4, :].rearrange("p (i g) c -> p i (g c)", g=2),
                                         op0=ALU.max, op1=ALU.add).then_inc(s_ke, 1)

            key_clip(0)
            for u in range(2 * NG):
                if u + 1 < 2 * NG:
                    key_clip(u + 1)
                key_sum(u)
            for g in range(NG):
                dve.wait_ge(s_q, g + 1)
                q = PS[6 + g % 2][:, :]
                d = grp(D, g).rearrange("p t c -> p (t c)")
                dve.tensor_scalar(d, q, 0.0, None, ALU.min).then_inc(s_qm, 1)
                dve.wait_ge(s_qx, g + 1)
                dve.scalar_tensor_tensor(out=pairs(QT, g), in0=q, scalar=0.0, in1=d, op0=ALU.max, op1=ALU.add).then_inc(s_qe, 1)
            for u in range(B // 4):
                dve.wait_ge(s_c, u + 1)
                src = PS[u % 6][:, :].rearrange("p (b c) -> p b c", b=4)
                for g in range(2):
                    mask = MASK[:, g:g + 1, :].broadcast_to((128, 4, C))
                    kvm = KVM[:, u * 4:u * 4 + 4, g, :]
                    dve.tensor_tensor(kvm[:, :, 0:64], src[:, :, 0:64], mask, ALU.mult).then_inc(s_ce, 1)
                    dve.tensor_tensor(kvm[:, :, 64:128], src[:, :, 64:65].broadcast_to((128, 4, 64)), mask,
                                      ALU.mult).then_inc(s_ce, 1)
            for u in range(NT // 4):
                dve.wait_ge(s_m, u + 1)
                src = PS[u % 6][:, :].rearrange("p (t c) -> p t c", t=4)
                e = E[:, u * 4:u * 4 + 4, :]
                step(dve.tensor_scalar(e, src[:, :, 64:128], ATT_EPS, None, ALU.add))
                step(dve.reciprocal(e, e))
                dve.scalar_tensor_tensor(out=MS[:, u * 4:u * 4 + 4, :], in0=src[:, :, 0:64], scalar=float(L), in1=e,
                                         op0=ALU.mult, op1=ALU.mult).then_inc(s_me, 1)
            dve.wait_ge(s_mte, NG)
            norm(1, bank, s_p, MS, s_pn, gain=0)
            norm(2, bank, s_o, MS, s_pn2, gain=2)
            dve.wait_ge(s_pn2, NG)
            for g in range(NG):
                step(dve.tensor_tensor(grp(HT, g), grp(HT, g), grp(XN, g), ALU.add))
                step(dve.tensor_tensor(grp(HT, g), grp(HT, g), grp(MS, g), ALU.add))
            dve.tensor_scalar(WA[:, :], WF[:, :], LNW[:, 0:1], None, ALU.mult).then_inc(s_wf, 1)
            dve.tensor_copy(LNBR[:, :], LNB[:, 0:1].broadcast_to((64, 128))).then_inc(s_wf, 1)
            dve.wait_ge(s_wf, 3)
            step(dve.tensor_copy(RW[:, :, 0:64], PS[6][:, 0:128].rearrange("p (g c) -> p g c", g=2)))
            step(dve.tensor_copy(RW[:, :, 64], MC[:, :]))
            step(dve.tensor_tensor(BF[:, :], PS[7][:, 0:64], GB[:, 4, :], ALU.add))
            dve.nop().then_inc(s_wfe, 1)
            norm(3, lambda g: grp(HT, g), None, XN, s_xn)

            def part(x, k):
                return x[:, k * PT:(k + 1) * PT, :]

            def nudge(m, k):
                dve.wait_ge(s_th, m + 1)
                dve.scalar_tensor_tensor(out=part(D, k), in0=part(D, k), scalar=0.01, in1=part(XN, k), op0=ALU.mult,
                                         op1=ALU.add).then_inc(s_hp, 1)

            def rescale(m, k):
                count = [0]

                def do(instruction):
                    instruction.then_inc(s_fs, 1)
                    count[0] += 1
                    dve.wait_ge(s_fs, m * SMALL2 + count[0])

                def st(i):
                    return ST[:, i, k * PT:(k + 1) * PT]

                dve.wait_ge(s_v, m + 1)
                do(dve.tensor_scalar(st(2), st(2), 0.0, C * EPS, ALU.max, ALU.add))
                rsqrt(st(2), st(3), st(6), st(5), do, float(C) ** 0.5)
                r = st(3).rearrange("p (b j o) -> p b j o", b=2, o=1).broadcast_to((128, 2, 6, C))
                assert count[0] == SMALL2, count[0]
                dve.tensor_tensor(part(XN, k).rearrange("p (b j) c -> p b j c", b=2), FY[k % 2][:, :, :, 0:64], r,
                                  ALU.mult).then_inc(s_sc, 1)

            def sum_squares(m, k):
                dve.wait_ge(s_s2, m + 1)
                dve.tensor_reduce(ST[:, 1, k * PT:(k + 1) * PT], part(E, k), axis=AX.X, op=ALU.add).then_inc(s_rd, 1)

            def quarter(m, k, before, first=False):
                nudge(m, k)
                if not first:
                    sum_squares(m - 1, (k - 1) % PARTS)
                if before:
                    rescale(m - 2, (k - 2) % PARTS)

            dve.nop().then_inc(s_sc, SC_CREDIT)
            for k in range(PARTS):
                quarter(k, k, k >= 2, first=(k == 0))
            with dve.Fori(1, ITERS) as n:
                for k in range(PARTS):
                    quarter(PARTS * n + k, k, True)
            sum_squares(PARTS * ITERS - 1, PARTS - 1)
            for k in range(2, PARTS):
                rescale(PARTS * (ITERS - 1) + k, k)
            dve.wait_ge(s_r, PARTS * (ITERS + 1))
            for g in range(NG):
                dve.tensor_tensor(grp(HT, g), grp(HT, g), grp(XN, g), ALU.add).then_inc(s_fin, 1)


def constants():
    f = 2 * np.pi / 64
    ky = np.arange(16)
    kx = np.concatenate([np.arange(16), np.arange(-16, 0)])
    w = np.arange(64)
    c1 = np.zeros((4, 32, 2, 4, 2, 16))
    ang = f * np.outer(w, ky).reshape(2, 32, 16)
    for cb in range(4):
        c1[cb, :, :, cb, 0] = np.cos(ang).transpose(1, 0, 2)
        c1[cb, :, :, cb, 1] = -np.sin(ang).transpose(1, 0, 2)
    ang = f * np.outer(w, kx).reshape(2, 32, 32)
    cs, sn = np.cos(ang), np.sin(ang)
    c2 = np.zeros((32, 2, 2, 2, 2, 2, 32))
    for z in range(2):
        for hh in range(2):
            c2[:, z, hh, 0, 0, z] = cs[hh]
            c2[:, z, hh, 1, 0, z] = sn[hh]
            c2[:, z, hh, 0, 1, z] = sn[hh]
            c2[:, z, hh, 1, 1, z] = -cs[hh]
    c3 = np.zeros((2, 32, 2, 2, 2, 2, 32))
    for bp in range(2):
        for hh in range(2):
            c3[bp, :, 0, bp, 0, hh] = cs[hh].T
            c3[bp, :, 1, bp, 0, hh] = -sn[hh].T
            c3[bp, :, 0, bp, 1, hh] = sn[hh].T
            c3[bp, :, 1, bp, 1, hh] = cs[hh].T
    kk = np.arange(16)
    order = (kk % 2) * 8 + kk // 2
    wt = np.where(order == 0, 1.0, 2.0)[:, None] / 4096
    ang = f * np.outer(order, w)
    c4 = np.zeros((2, 2, 2, 16, 2, 2, 64))
    for z in range(2):
        for hh in range(2):
            c4[0, hh, z, :, z, hh] = wt * np.cos(ang)
            c4[1, hh, z, :, z, hh] = -wt * np.sin(ang)
    p = np.arange(128)
    avg = (p[:, None] % 64 == p[None, :] % 64) * 0.5
    heads = (np.arange(64)[:, None] // 8 == np.arange(64)[None, :] // 8) * 1.0
    heads = np.stack([np.concatenate([heads, 0 * heads]), np.concatenate([0 * heads, heads])], 1)
    center = np.eye(128) - (p[:, None] // 64 == p[None, :] // 64) / 64
    meancol = (p[:, None] // 64 == np.arange(2)[None, :]) / 64
    r = lambda a, *s: np.ascontiguousarray(a.reshape(s), dtype=np.float32)
    return {"c1": r(c1, 128, 2, 128), "c2": r(c2, 128, 2, 128), "c3": r(c3, 128, 2, 128), "c4": r(c4, 128, 256),
            "ident": r(np.eye(128), 128, 128), "avg": r(avg, 128, 128),
            "heads": r(heads, 128, 2, 64), "halves": r(p[:, None] // 64 == np.arange(2)[None, :], 128, 2), "center": r(center, 128, 128), "meancol": r(meancol, 128, 2)}


def laid_out(i):
    g = {k: np.asarray(v) for k, v in i.items()}
    x = g["x"].reshape(8, 2, 2, 2, 8, 4, 64, 3).transpose(0, 4, 2, 7, 5, 1, 3, 6).reshape(4, 128, 768)
    def pack(a):
        return np.asarray(a).reshape(4, 64, 64, 4, 4, 16).transpose(0, 3, 1, 4, 5, 2)
    top = np.stack([pack(g["L0_tok_w1r"]), pack(g["L0_tok_w1i"])], 2)
    bot = np.stack([pack(g["L0_tok_w2r"]), pack(g["L0_tok_w2i"])], 2)
    modew = np.stack([top, bot], 1).reshape(32, 128, 4096)
    c = np.ascontiguousarray
    return {"x": c(x), "txt": g["txt"], "modew": c(modew),
            "fc0_w": g["L0_tok_fc0_w"], "fc0_b": g["L0_tok_fc0_b"].reshape(64, 1),
            "pw_w": c(g["L0_tok_pw_w"].transpose(0, 2, 1)),
            "prm": c(np.stack([g["L0_tok_gamma"], g["L0_tok_beta"], g["L0_tok_pw_b"]], -1)),
            "fc1_w": g["L0_tok_fc1_w"], "fc1_b": g["L0_tok_fc1_b"].reshape(128, 1),
            "fc2_w": g["L0_tok_fc2_w"], "fc2_b": g["L0_tok_fc2_b"].reshape(1, 1),
            **{k: g["L0_attn_" + k] for k in ("Wq", "Wk", "Wv", "Wm", "W1", "W2")},
            **{k: g["L0_attn_" + k].reshape(1, 64) for k in ("g1", "b1", "g2", "b2")},
            "ln_w": g["L0_ffn_ln_w"].reshape(64, 1), "ln_b": g["L0_ffn_ln_b"].reshape(64, 1),
            "ffn_wt": c(g["L0_ffn_W"].T), "ffn_b": g["L0_ffn_b"].reshape(1, 64)}


def kernel(**inputs):
    import numpy as np
    import concourse.bacc as bacc
    from concourse import mybir
    from concourse.bass_utils import run_bass_kernel_spmd as run

    nc = bacc.Bacc("TRN2", target_bir_lowering=False, num_devices=1)
    F32 = mybir.dt.float32
    arrays, t = {}, {}
    for name, a in {**constants(), **laid_out(inputs)}.items():
        arrays[f"in_{name}"] = np.ascontiguousarray(a)
        t[name] = nc.dram_tensor(f"in_{name}", arrays[f"in_{name}"].shape, F32, kind="ExternalInput").ap()
    out = nc.dram_tensor("out_tokens", [B, H + TXT, C], F32, kind="ExternalOutput").ap()
    hcat = nc.dram_tensor("token_scratch", [B, H + TXT, C], F32, kind="Internal").ap()
    build_tokenizer(nc, t, hcat)
    build_mixer(nc, t, hcat, out)
    r = run(nc, [arrays], core_ids=[0])
    return r.results[0]["out_tokens"]
```
